# Optimizing a Trainium2 kernel written in Bass

```python
import numpy as np
import jax
import jax.numpy as jnp

def _softmax(x, axis=-1):
    return jax.nn.softmax(x, axis=axis)

def _gelu(x):
    return jax.nn.gelu(x, approximate=True)

def _silu(x):
    return jax.nn.silu(x)

def _sigmoid(x):
    return jax.nn.sigmoid(x)

def _layernorm(x, axis=-1, eps=1e-05):
    m = jnp.mean(x, axis=axis, keepdims=True)
    v = jnp.var(x, axis=axis, keepdims=True)
    return (x - m) / jnp.sqrt(v + eps)

def _scatter_add(tgt, idx, src, axis=0):
    return tgt.at[idx].add(src)

def _segment_sum(src, seg, n):
    return jax.ops.segment_sum(src, seg, n)
kernel_name = 'mk_decoder_preln_d1_seqx_r4_41ae4d'

def setup_inputs(seed: int=0):
    np.random.seed(seed)
    _w = jnp.asarray

    def _rec_inputs():
        import jax
        import jax.numpy as jnp
        _rk = jax.random.key(seed)
        x = -0.0003929 + 0.9999 * jax.random.normal(jax.random.fold_in(_rk, 1), (8, 512, 256), jnp.float32)
        _lenS = 512 - jax.random.randint(jax.random.fold_in(_rk, 7), (8,), 0, max(1, 512 // 4) + 1, jnp.int32)
        _lenS2 = 64 - jax.random.randint(jax.random.fold_in(_rk, 8), (8,), 0, max(1, 64 // 4) + 1, jnp.int32)
        _ctx_1024P = jax.random.normal(jax.random.fold_in(_rk, 11), (8, 16, 256), jnp.float32)
        _ctx_1024c = jax.random.dirichlet(jax.random.fold_in(_rk, 511), 0.3 * jnp.ones((16,), jnp.float32), (8, 64))
        _ctx_1024t = jnp.einsum('bsk,bkd->bsd', _ctx_1024c, _ctx_1024P)
        _ctx_1024t = _ctx_1024t * jax.lax.rsqrt(jnp.mean(jnp.square(_ctx_1024t)) + 1e-12) * 0.953939
        ctx_1024 = 2.81802e-05 + 1.00001 * (_ctx_1024t + 0.3 * jax.random.normal(jax.random.fold_in(_rk, 611), (8, 64, 256), jnp.float32))
        _validS = jnp.arange(512)[None, :] < _lenS[:, None]
        _validS2 = jnp.arange(64)[None, :] < _lenS2[:, None]
        _causal = jnp.tril(jnp.ones((512, 512), dtype=bool))
        mask_SxS2_ik1 = jnp.where(jnp.broadcast_to(_validS2[0:1, :], (512, 64)), 1, 0).astype(jnp.int32)
        return (x, ctx_1024, mask_SxS2_ik1)
    x, ctx_1024, mask_SxS2_ik1 = _rec_inputs()

    def _L0_attn_setup():
        import jax, jax.numpy as jnp
        import numpy as np
        import math
        B, T, C = (4, 512, 256)
        H, DQK, DV = (16, 64, 64)
        key = jax.random.key(seed)
        k1, k2, k3, k4, k5 = jax.random.split(key, 5)
        x_q = jax.random.normal(k1, (B, T, C), dtype=jnp.float32)
        w_q = jax.random.normal(k2, (H, DQK, C), dtype=jnp.float32) / math.sqrt(C)
        w_k = jax.random.normal(k3, (H, DQK, C), dtype=jnp.float32) / math.sqrt(C)
        w_v = jax.random.normal(k4, (H, DV, C), dtype=jnp.float32) / math.sqrt(C)
        w_o = jax.random.normal(k5, (DV * H, C), dtype=jnp.float32) / math.sqrt(C)
        return {'x_q': x_q, 'w_q': w_q, 'w_k': w_k, 'w_v': w_v, 'w_o': w_o}
    _L0_attn_all = _L0_attn_setup()
    _L0_attn_in = {k: v for k, v in _L0_attn_all.items() if k in ('w_q', 'w_k', 'w_v', 'w_o')}
    del _L0_attn_all

    def _L0_xattn_setup():
        import jax, jax.numpy as jnp
        import numpy as np
        B, N, M, D_MODEL, D_K, D_V = (8, 512, 512, 256, 256, 256)
        NEG = -1000000000.0
        key = jax.random.key(seed)
        ks = jax.random.split(key, 10)
        s = 1.0 / np.sqrt(D_MODEL)
        return {'querys': jax.random.normal(ks[0], (B, N, D_MODEL), jnp.float32), 'keys': jax.random.normal(ks[1], (B, M, D_MODEL), jnp.float32), 'values': jax.random.normal(ks[2], (B, M, D_MODEL), jnp.float32), 'mask': jax.random.randint(ks[3], (N, M), 0, 2, jnp.int32), 'Wq': jax.random.normal(ks[4], (D_K, D_MODEL), jnp.float32) * s, 'bq': jnp.zeros((D_K,), jnp.float32), 'Wk': jax.random.normal(ks[5], (D_K, D_MODEL), jnp.float32) * s, 'bk': jnp.zeros((D_K,), jnp.float32), 'Wv': jax.random.normal(ks[6], (D_V, D_MODEL), jnp.float32) * s, 'bv': jnp.zeros((D_V,), jnp.float32)}
    _L0_xattn_all = _L0_xattn_setup()
    _L0_xattn_in = {k: v for k, v in _L0_xattn_all.items() if k in ('Wq', 'bq', 'Wk', 'bk', 'Wv', 'bv')}
    del _L0_xattn_all

    def _L0_ffn_setup():
        import jax, jax.numpy as jnp
        import numpy as np
        D_IN, D_HID = (256, 1024)

        def _ternary(key, shape):
            return jax.random.randint(key, shape, -1, 2).astype(jnp.float32)

        def _tlin(x, w, s):
            return jnp.einsum('bsi,oi->bso', x, w) * s
        key = jax.random.key(seed)
        ks = jax.random.split(key, 12)
        inv = lambda fan: 1.0 / np.sqrt(fan).astype(np.float32)
        return {'x': jax.random.normal(ks[0], (4, 512, D_IN), dtype=jnp.float32), 'w1_w': _ternary(ks[1], (D_HID, D_IN)), 'w1_s': jax.random.uniform(ks[2], (D_HID,), dtype=jnp.float32) * inv(D_IN), 'w2_w': _ternary(ks[3], (D_HID, D_IN)), 'w2_s': jax.random.uniform(ks[4], (D_HID,), dtype=jnp.float32) * inv(D_IN), 'h1_w': _ternary(ks[5], (D_HID, D_HID)), 'h1_s': jax.random.uniform(ks[6], (D_HID,), dtype=jnp.float32) * inv(D_HID), 'h2_w': _ternary(ks[7], (D_HID, D_HID)), 'h2_s': jax.random.uniform(ks[8], (D_HID,), dtype=jnp.float32) * inv(D_HID), 'w3_w': _ternary(ks[9], (D_IN, D_HID)), 'w3_s': jax.random.uniform(ks[10], (D_IN,), dtype=jnp.float32) * inv(D_HID)}
    _L0_ffn_all = _L0_ffn_setup()
    _L0_ffn_in = {k: v for k, v in _L0_ffn_all.items() if k in ('w1_w', 'w1_s', 'w2_w', 'w2_s', 'h1_w', 'h1_s', 'h2_w', 'h2_s', 'w3_w', 'w3_s')}
    del _L0_ffn_all
    return {'x': x, 'ctx_1024': ctx_1024, 'mask_SxS2_ik1': mask_SxS2_ik1, 'L0_attn_w_q': _L0_attn_in['w_q'], 'L0_attn_w_k': _L0_attn_in['w_k'], 'L0_attn_w_v': _L0_attn_in['w_v'], 'L0_attn_w_o': _L0_attn_in['w_o'], 'L0_xattn_Wq': _L0_xattn_in['Wq'], 'L0_xattn_bq': _L0_xattn_in['bq'], 'L0_xattn_Wk': _L0_xattn_in['Wk'], 'L0_xattn_bk': _L0_xattn_in['bk'], 'L0_xattn_Wv': _L0_xattn_in['Wv'], 'L0_xattn_bv': _L0_xattn_in['bv'], 'L0_ffn_w1_w': _L0_ffn_in['w1_w'], 'L0_ffn_w1_s': _L0_ffn_in['w1_s'], 'L0_ffn_w2_w': _L0_ffn_in['w2_w'], 'L0_ffn_w2_s': _L0_ffn_in['w2_s'], 'L0_ffn_h1_w': _L0_ffn_in['h1_w'], 'L0_ffn_h1_s': _L0_ffn_in['h1_s'], 'L0_ffn_h2_w': _L0_ffn_in['h2_w'], 'L0_ffn_h2_s': _L0_ffn_in['h2_s'], 'L0_ffn_w3_w': _L0_ffn_in['w3_w'], 'L0_ffn_w3_s': _L0_ffn_in['w3_s']}

def reference(x, ctx_1024, mask_SxS2_ik1, L0_attn_w_q, L0_attn_w_k, L0_attn_w_v, L0_attn_w_o, L0_xattn_Wq, L0_xattn_bq, L0_xattn_Wk, L0_xattn_bk, L0_xattn_Wv, L0_xattn_bv, L0_ffn_w1_w, L0_ffn_w1_s, L0_ffn_w2_w, L0_ffn_w2_s, L0_ffn_h1_w, L0_ffn_h1_s, L0_ffn_h2_w, L0_ffn_h2_s, L0_ffn_w3_w, L0_ffn_w3_s):
    import jax
    import jax.numpy as jnp

    def _L0_attn_ref(x_q, w_q, w_k, w_v, w_o):
        import jax, jax.numpy as jnp
        import numpy as np
        import math
        B, T, C = (4, 512, 256)
        H, DQK, DV = (16, 64, 64)
        q = jnp.einsum('ntc,hdc->nhtd', x_q, w_q)
        k = jnp.einsum('ntc,hdc->nhtd', x_q, w_k)
        v = jnp.einsum('ntc,hdc->nhtd', x_q, w_v)
        a = jnp.einsum('nhtd,nhsd->nhts', q, k) / math.sqrt(q.shape[3])
        t = a.shape[2]
        causal_forbidden = jnp.arange(t)[:, None] < jnp.arange(t)[None, :]
        a = jnp.where(causal_forbidden[None, None], -jnp.inf, a)
        a = jax.nn.softmax(a, axis=3)
        y = jnp.einsum('nhts,nhsd->nthd', a, v).reshape(a.shape[0], t, -1)
        return y @ w_o

    def _L0_xattn_ref(querys, keys, values, mask, Wq, bq, Wk, bk, Wv, bv):
        import jax, jax.numpy as jnp
        import numpy as np
        B, N, M, D_MODEL, D_K, D_V = (8, 512, 512, 256, 256, 256)
        NEG = -1000000000.0
        q = querys @ Wq.T + bq
        k = keys @ Wk.T + bk
        v = values @ Wv.T + bv
        scores = jnp.einsum('bnd,bmd->bnm', q, k)
        scores = jnp.where(mask[None, :, :] == 0, NEG, scores)
        weights = jax.nn.softmax(scores, axis=2)
        out = jnp.einsum('bnm,bmd->bnd', weights, v)
        return out

    def _L0_ffn_ref(x, w1_w, w1_s, w2_w, w2_s, h1_w, h1_s, h2_w, h2_s, w3_w, w3_s):
        import jax, jax.numpy as jnp
        import numpy as np
        D_IN, D_HID = (256, 1024)

        def _ternary(key, shape):
            return jax.random.randint(key, shape, -1, 2).astype(jnp.float32)

        def _tlin(x, w, s):
            return jnp.einsum('bsi,oi->bso', x, w) * s
        h = jax.nn.silu(_tlin(x, w1_w, w1_s)) * _tlin(x, w2_w, w2_s)
        h = jax.nn.gelu(_tlin(h, h1_w, h1_s), approximate=False)
        h = jax.nn.gelu(_tlin(h, h2_w, h2_s), approximate=False)
        return _tlin(h, w3_w, w3_s)
    x = x + _L0_attn_ref(_layernorm(x, axis=-1), L0_attn_w_q, L0_attn_w_k, L0_attn_w_v, L0_attn_w_o)
    x = x + _L0_xattn_ref(_layernorm(x, axis=-1), ctx_1024, ctx_1024, mask_SxS2_ik1, L0_xattn_Wq, L0_xattn_bq, L0_xattn_Wk, L0_xattn_bk, L0_xattn_Wv, L0_xattn_bv)
    x = x + _L0_ffn_ref(_layernorm(x, axis=-1), L0_ffn_w1_w, L0_ffn_w1_s, L0_ffn_w2_w, L0_ffn_w2_s, L0_ffn_h1_w, L0_ffn_h1_s, L0_ffn_h2_w, L0_ffn_h2_s, L0_ffn_w3_w, L0_ffn_w3_s)
    return x

_drawn_inputs = setup_inputs


def setup_inputs(seed=0):
    import zlib

    import numpy as np

    out = dict(_drawn_inputs(seed))
    spreads = {'L0_xattn_bq': (0.0, 0.1), 'L0_xattn_bk': (0.0, 0.1), 'L0_xattn_bv': (0.0, 0.1)}
    factors = {}
    for name, (base, spread) in spreads.items():
        noise = np.random.default_rng([zlib.crc32(name.encode()), seed]).standard_normal(out[name].shape)
        drawn = base * np.exp(spread * noise) if base else spread * noise
        out[name] = jnp.asarray(drawn.astype(out[name].dtype))
    for name, factor in factors.items():
        out[name] = (out[name] * factor).astype(out[name].dtype)
    return out
```

```python
import concourse.bass as bass
from concourse import mybir
from contextlib import ExitStack


class Chan:

    def __init__(self, sem, step=1):
        self.sem, self.step, self.n = sem, step, 0


class Queues:

    def __init__(self):
        self.q = {k: [] for k in ("tensor", "vector", "scalar", "gpsimd", "sync")}
        self.seen = {k: {} for k in self.q}

    def wait(self, eng, events):
        for ev in events:
            if ev is None:
                continue
            ch, n = ev
            if self.seen[eng].get(ch, 0) < n:
                self.seen[eng][ch] = n
                self.q[eng].append(lambda e, ch=ch, n=n: e.wait_ge(ch.sem, n))

    def put(self, eng, fn, waits=(), sig=None):
        self.wait(eng, waits)
        if sig is None:
            self.q[eng].append(fn)
            return None
        sig.n += sig.step
        self.q[eng].append(lambda e: fn(e).then_inc(sig.sem, sig.step))
        return (sig, sig.n)


class Ring:

    def __init__(self, tiles):
        self.tiles, self.free, self.i = tiles, [[] for _ in tiles], -1

    def take(self):
        self.i += 1
        k = self.i % len(self.tiles)
        f, self.free[k] = self.free[k], None
        assert f is not None
        return k, self.tiles[k], f


B, T, C, H = 8, 512, 256, 16
NT = 4
S2 = 64
NEG = -1e30
EPS = 1e-5


def program(nc, A, out):
    f32, f32r, i32 = mybir.dt.float32, mybir.dt.float32r, mybir.dt.int32
    ACT, ALU, AX = mybir.ActivationFunctionType, mybir.AluOpType, mybir.AxisListType
    Q = Queues()
    put = Q.put
    root = ExitStack()
    x1_d = nc.dram_tensor("x1_scratch", (B, T, C), f32, kind="Internal").ap()
    x2_d = nc.dram_tensor("x2_scratch", (B, T, C), f32, kind="Internal").ap()
    h_d = nc.dram_tensor("h_scratch", (B, 8, 128, T), f32, kind="Internal").ap()
    sems = {}

    def chan(name, step=1):
        if name not in sems:
            sems[name] = Chan(root.enter_context(nc.semaphore(name)), step)
        return sems[name]

    def dma(dst, src, name, waits=()):
        return put("sync", lambda e: e.dma_start(dst, src), waits, chan(name, 16))

    psum = [root.enter_context(nc.psum_tensor(f"bank{i}", [128, 512], f32)) for i in range(8)]

    def sbf(cx, name, shape, dt=f32):
        return cx.enter_context(nc.sbuf_tensor(name, shape, dt))

    ident = sbf(root, "ident", [128, 128])
    identr = sbf(root, "identr", [128, 128], f32r)
    s_c = chan("s_const")
    e0 = put("gpsimd", lambda e: e.memset(ident[:, :], 0.0), (), s_c)
    e_id = put("gpsimd", lambda e: e.affine_select(out=ident[:, :], in_=ident[:, :], compare_op=ALU.not_equal,
               fill=1.0, base=0, pattern=[[-1, 128]], channel_multiplier=1), [e0], s_c)
    e_idr = put("scalar", lambda e: e.activation(identr[:, :], ident[:, :], ACT.Copy), [e_id], chan("s_identr"))

    def copy(eng, dst, src, waits, sig, scale=1.0):
        if eng == "scalar":
            return put(eng, lambda e: e.activation(dst, src, ACT.Copy, scale=scale), waits, sig)
        return put(eng, lambda e: e.tensor_scalar(dst, src, scale, 1.0, ALU.mult, ALU.mult), waits, sig)

    def minus(eng, dst, a, b, waits, sig):
        return put(eng, lambda e: e.tensor_tensor(dst, a, b.bitcast(f32), ALU.subtract), waits, sig)

    stage_n = [0]

    def split_weight(ring, dst_hi, dst_lo, src, n, scale=1.0, waits=(), eng=("scalar", "vector")):
        evs = []
        for a in range(0, n, 1024):
            m = min(1024, n - a)
            k, st, free = ring.take()
            e_ld = dma(st[:, 0:m], src[:, a:a + m], f"s_wld{k}", list(free) + list(waits))
            if scale != 1.0:
                e_ld = put("gpsimd", lambda e, st=st, m=m: e.tensor_scalar(
                    st[:, 0:m], st[:, 0:m], scale, 1.0, ALU.mult, ALU.mult), [e_ld], chan("s_wscale"))
            e_hi = copy(eng[0], dst_hi[:, a:a + m], st[:, 0:m], [e_ld] + list(waits), chan("s_whi_" + eng[0]))
            e_lo = minus(eng[1], dst_lo[:, a:a + m], st[:, 0:m], dst_hi[:, a:a + m], [e_hi],
                         chan("s_wlo_" + eng[1]))
            ring.free[k] = [e_lo]
            evs += [e_lo]
        return evs

    def mm3(dst, whi, wlo, xhi, xlo, first, last, waits, sig):
        put("tensor", lambda e: e.matmul(dst, whi, xhi, start=first, stop=False), waits)
        put("tensor", lambda e: e.matmul(dst, whi, xlo, start=False, stop=False))
        return put("tensor", lambda e: e.matmul(dst, wlo, xhi, start=False, stop=last), (), sig)

    def layernorm(tag, x, xn, small, waits, free):
        st = small[:, :, 0:6]
        mv = small[:, :, 6:8]
        rs = small[:, :, 8:9]
        s = chan("s_ln")
        for t in range(NT):
            ev = put("vector", lambda e, t=t: e.bn_stats(st[:, t, :], x[:, t, :]), list(waits) + list(free), s)
        for t in range(NT):
            ev = put("vector", lambda e, t=t: e.bn_aggr(mv[:, t, :], st[:, t, :]), [ev], s)
        ev = put("vector", lambda e: e.tensor_scalar(rs, mv[:, :, 1:2], EPS, None, ALU.add), [ev], s)
        ev = put("gpsimd", lambda e: e.tensor_tensor(rs, rs, half[:, :].rearrange("p (t o) -> p t o", o=1), ALU.pow),
                 [ev, e_half], chan("s_rstd"))
        for t in range(NT):
            ev2 = put("vector", lambda e, t=t: e.tensor_scalar(xn[:, t, :], x[:, t, :], mv[:, t, 0:1], rs[:, t, :],
                      ALU.subtract, ALU.mult), [ev], s)
        return ev2

    def transpose_split(xn, e_xn, XT, free, ring, j):
        k, bank, bf = ring.take()
        for t in range(NT):
            ev = put("tensor", lambda e, t=t: e.transpose(bank[:, t * 128:t * 128 + 128],
                     xn[:, t, j * 128:j * 128 + 128], ident[:, :]), [e_xn, e_id] + list(bf),
                     chan("s_xnT") if t == NT - 1 else None)
        e_hi = copy("scalar", XT[:, 0, j, :], bank[:, :], [ev] + list(free), chan("s_xhi"))
        e_lo = minus("vector", XT[:, 1, j, :], bank[:, :], XT[:, 0, j, :], [e_hi] + list(free), chan("s_xlo"))
        ring.free[k] = [e_lo]
        return e_lo

    half = sbf(root, "half", [128, NT])
    e_half = put("gpsimd", lambda e: e.memset(half[:, :], -0.5), (), s_c)

    cx = ExitStack()
    cmask = sbf(cx, "cmask", [128, 128])
    cmaskr = sbf(cx, "cmaskr", [128, 128], f32r)
    e0 = put("gpsimd", lambda e: e.memset(cmask[:, :], 0.0), (), s_c)
    e0 = put("gpsimd", lambda e: e.affine_select(out=cmask[:, :], in_=cmask[:, :], compare_op=ALU.is_ge, fill=NEG,
             base=0, pattern=[[-1, 128]], channel_multiplier=1), [e0], s_c)
    e_cm = put("scalar", lambda e: e.activation(cmaskr[:, :], cmask[:, :], ACT.Copy), [e0], chan("s_identr"))
    Wq = sbf(cx, "Wq", [128, 2, 2, 1024], f32r)
    Wk = sbf(cx, "Wk", [128, 2, 2, 1024], f32r)
    Wv = sbf(cx, "Wv", [128, 2, 2, 1024], f32r)
    Wo = sbf(cx, "Wo", [128, 2, 8, 256], f32r)
    XTb = [sbf(cx, f"XT{i}", [128, 2, 2, 512], f32r) for i in range(2)]
    Kb = Ring([sbf(cx, f"K{i}", [128, 2, 512], f32r) for i in range(2)])
    Qb = Ring([sbf(cx, f"Qz{i}", [128, 2, 2, 512], f32r) for i in range(2)])
    Vb = Ring([sbf(cx, f"V{i}", [128, NT, 4, 256], f32r) for i in range(2)])
    Pb = Ring([sbf(cx, f"P{i}", [128, 1280]) for i in range(2)])
    PTb = Ring([sbf(cx, f"PT{i}", [128, 2, 1280], f32r) for i in range(2)])
    Yb = Ring([sbf(cx, f"Y{i}", [128, 2, 512], f32r) for i in range(4)])
    Yf = Ring([sbf(cx, "Yf0", [128, 512])])
    tmpb = Ring([sbf(cx, "ytmp", [128, 512])])
    xb = [sbf(cx, f"x{i}", [128, NT, 256]) for i in range(2)]
    xn = sbf(cx, "xn", [128, NT, 256])
    small = sbf(cx, "lnsmall", [128, NT, 9])
    stats = [sbf(cx, f"stats{i}", [128, 12]) for i in range(4)]
    stage = Ring([Pb.tiles[0][:, 0:1024], Pb.tiles[1][:, 0:1024], xb[1][:, :, :].rearrange("p t c -> p (t c)")])

    x_in = A["x"].rearrange("b (t p) c -> b p t c", p=128)
    x1_v = x1_d.rearrange("b (t p) c -> b p t c", p=128)
    x2_v = x2_d.rearrange("b (t p) c -> b p t c", p=128)
    out_v = out.rearrange("b (t p) c -> b p t c", p=128)

    Sr = Ring([psum[i] for i in (0, 1, 2)])
    Tr = Ring([psum[i] for i in (3, 4)])
    Or = Ring([psum[5]])
    Gr = Ring([psum[i] for i in (6, 7)])

    e_x = {0: dma(xb[0][:, :, :], x_in[0], "s_xld0")}
    flat = lambda w, i: w[:, i, :, :].rearrange("p k f -> p (k f)")
    e_wq = split_weight(stage, flat(Wq, 0), flat(Wq, 1), A["wq"], 2048, scale=0.125)
    e_wk = split_weight(stage, flat(Wk, 0), flat(Wk, 1), A["wk"], 2048)
    e_wv = split_weight(stage, flat(Wv, 0), flat(Wv, 1), A["wv"], 2048)
    e_wo = split_weight(stage, flat(Wo, 0), flat(Wo, 1), A["wo"], 2048)
    for i in range(2):
        Pb.free[i] = list(stage.free[i])
    e_x1free = list(stage.free[2])

    for i, q in enumerate(Qb.tiles):
        for a, (lo_p, hi_p) in enumerate(((64, 128), (0, 64))):
            for k in range(2):
                ev = put("vector", lambda e, q=q, a=a, k=k, lo_p=lo_p, hi_p=hi_p: e.memset(
                    q[lo_p:hi_p, a, k, :].bitcast(f32), 0.0), (), chan("s_qzero"))
    e_qz = ev

    bg = []
    done = set()

    def run_bg(n):
        for _ in range(n):
            if bg:
                tag, fn = bg.pop(0)
                fn()
                done.add(tag)

    def need(tag):
        while tag not in done:
            assert bg, tag
            run_bg(1)

    e_XT, XT_free, e_xacc = {}, [[], []], {}
    pairQ, pairK, halfV = {}, {}, {}

    def ln1(b):
        def load():
            if b not in e_x:
                e_x[b] = dma(xb[b % 2][:, :, :], x_in[b], f"s_xld{b % 2}",
                             e_x1free if b == 1 else [e_st1[b - 2]])
        def norm():
            load()
            e_xn[b] = layernorm("l1", xb[b % 2], xn, small, [e_x[b]], [e_XT[b - 1][1]] if b else [])
        def tr(j):
            ev = transpose_split(xn, e_xn[b], XTb[b % 2], XT_free[b % 2], Gr, j)
            e_XT.setdefault(b, []).append(ev)
        return [(("ln", b), norm), (("xt0", b), lambda: tr(0)), (("xt", b), lambda: tr(1))]
    e_xn, e_st1 = {}, {}

    def proj(P, which):
        b, p = P // 8, P % 8
        def go():
            X = XTb[b % 2]
            W, ew = (Wq, e_wq) if which == "q" else (Wk, e_wk)
            k, bank, bf = Gr.take()
            fs = slice(p * 128, p * 128 + 128)
            for c in range(2):
                ev = mm3(bank[:, :], W[:, 0, c, fs], W[:, 1, c, fs], X[:, 0, c, :], X[:, 1, c, :],
                         c == 0, c == 1, list(bf) + e_XT[b] + ew, chan("s_qk") if c == 1 else None)
            if which == "k":
                kb, Kt, kf = Kb.take()
                e1 = copy("scalar", Kt[:, 0, :], bank[:, :], [ev] + list(kf), chan("s_qkhi"))
                e2 = minus("vector", Kt[:, 1, :], bank[:, :], Kt[:, 0, :], [e1], chan("s_qklo"))
                pairK[P] = (kb, Kt, e2)
            else:
                qb, Qt, qf = Qb.take()
                for a in range(2):
                    r = slice(64 * a, 64 * a + 64)
                    e1 = copy("scalar", Qt[r, a, 0, :], bank[r, :], [ev, e_qz] + list(qf), chan("s_qkhi"))
                for a in range(2):
                    r = slice(64 * a, 64 * a + 64)
                    e2 = minus("vector", Qt[r, a, 1, :], bank[r, :], Qt[r, a, 0, :], [e1, e_qz] + list(qf),
                               chan("s_qklo"))
                pairQ[P] = (qb, Qt, e2)
            Gr.free[k] = [e2]
            if P % 8 == 7 and which == "k":
                XT_free[b % 2] = [ev]
        return ((which, P), go)

    def vproj(Hf, t):
        b, hh = Hf // 2, Hf % 2
        def go():
            if t == 0:
                halfV[Hf] = [*Vb.take(), None]
            kb, Vt, vf, _ = halfV[Hf]
            X = XTb[b % 2]
            k, bank, bf = Gr.take()
            ts = slice(t * 128, t * 128 + 128)
            fs = slice(hh * 512, hh * 512 + 512)
            for c in range(2):
                ev = mm3(bank[:, :], X[:, 0, c, ts], X[:, 1, c, ts], Wv[:, 0, c, fs], Wv[:, 1, c, fs],
                         c == 0, c == 1, list(bf) + e_XT[b] + e_wv, chan("s_v") if c == 1 else None)
            src = bank[:, :].rearrange("p (q a d) -> p q a d", q=4, a=2)
            v4 = Vt[:, t, :, :].rearrange("p q (s d) -> p q s d", d=64)
            e1 = copy("scalar", v4[:, :, 0:4:3, :], src, [ev] + list(vf), chan("s_vhi"))
            e2 = minus("vector", v4[:, :, 1:3, :], src, v4[:, :, 0:4:3, :], [e1] + list(vf), chan("s_vlo"))
            Gr.free[k] = [e2]
            halfV[Hf][3] = e2
        return (("v", Hf, t), go)

    Yslot = {}

    def oproj(Qr, tt):
        b = Qr // 4
        def go():
            k, bank, bf = Gr.take()
            n = 0
            for t in (2 * tt, 2 * tt + 1):
                o = bank[:, (t % 2) * 256:(t % 2) * 256 + 256]
                ts = slice(t * 128, t * 128 + 128)
                for i in range(2):
                    P = 2 * Qr + i
                    yk, Yt, ey = Yslot[P]
                    ev = mm3(o, Yt[:, 0, ts], Yt[:, 1, ts], Wo[:, 0, P % 8, :], Wo[:, 1, P % 8, :],
                             i == 0, i == 1, list(bf) + [ey] + e_wo, chan("s_o") if i == 1 else None)
            if tt == 1:
                for i in range(2):
                    Yb.free[Yslot[2 * Qr + i][0]] = [ev]
            xt = xb[b % 2][:, 2 * tt:2 * tt + 2, :].rearrange("p t c -> p (t c)")
            e2 = put("vector", lambda e: e.tensor_tensor(xt, xt, bank[:, :], ALU.add), [ev, e_xn[b]]
                     + ([e_xacc[b, tt]] if (b, tt) in e_xacc else []), chan("s_xacc"))
            Gr.free[k] = [e2]
            e_xacc[b, tt] = e2
            if Qr % 4 == 3 and tt == 1:
                e_st1[b] = dma(x1_v[b], xb[b % 2][:, :, :], f"s_x1st{b % 2}", [e2])
        return (("o", Qr, tt), go)

    OFF = {0: 0, 1: 512, 3: 896, 2: 1024}
    POFF = {3: 0, 2: 512, 1: 896, 0: 1152}
    hd = {}

    def scores(g, i):
        P, a = g // 2, g % 2
        if i == 3:
            need(("q", P)), need(("k", P))
            pk, Pt, pf = Pb.take()
            hd[g] = dict(P=(pk, Pt, pf), exp={})
        d = hd[g]
        qb, Qt, eq = pairQ[P]
        kb, Kt, ek = pairK[P]
        k, bank, bf = Sr.take()
        n = 128 * (i + 1)
        qs = slice(i * 128, i * 128 + 128)
        mm3(bank[:, 0:n], Qt[:, a, 0, qs], Qt[:, a, 1, qs], Kt[:, 0, 0:n], Kt[:, 1, 0:n], True, False,
            list(bf) + [eq, ek], None)
        ev = put("tensor", lambda e: e.matmul(bank[:, n - 128:n], identr[:, :], cmaskr[:, :], start=False,
                 stop=True), [e_idr, e_cm], chan("s_S"))
        if a == 1 and i == 0:
            Qb.free[qb] = [ev]
            Kb.free[kb] = [ev]
        st = stats[g % 4]
        e1 = put("vector", lambda e: e.tensor_reduce(st[:, i:i + 1], bank[:, 0:n], AX.X, ALU.max, negate=True),
                 [ev] + ([hd[g - 4]["norm"]] if g >= 4 else []), chan("s_max"))
        _, Pt, pf = d["P"]
        e2 = put("scalar", lambda e: e.activation(Pt[:, POFF[i]:POFF[i] + n], bank[:, 0:n], ACT.Exp,
                 bias=st[:, i:i + 1], scale=1.0, accum_out=st[:, 4 + i:5 + i]), [e1] + list(pf), chan("s_exp"))
        Sr.free[k] = [e2]
        d["exp"][i] = e2

    def normalise(g):
        d = hd[g]
        st = stats[g % 4]
        er = put("vector", lambda e: e.reciprocal(st[:, 8:12], st[:, 4:8]), [d["exp"][0]], chan("s_recip"))
        Pt = d["P"][1]
        d["nrm"] = {}
        for i in (3, 2, 1, 0):
            n = 128 * (i + 1)
            ev = put("gpsimd", lambda e, i=i, n=n: e.tensor_scalar(
                Pt[:, POFF[i]:POFF[i] + n], Pt[:, POFF[i]:POFF[i] + n], st[:, 8 + i:9 + i], 1.0,
                ALU.mult, ALU.mult), [er], chan("s_norm"))
        d["norm"] = ev

    GROUPS = [[0], [1, 3], [2]]

    def transposes(g, u):
        d = hd[g]
        pk, Pt, _ = d["P"]
        if u == 0:
            d["PT"] = PTb.take()
            d["pt_ev"] = []
        tk, PTt, tf = d["PT"]
        k, bank, bf = Tr.take()
        base = OFF[GROUPS[u][0]]
        at = 0
        for j in GROUPS[u]:
            for i in range(j, 4):
                ev = put("tensor", lambda e, i=i, j=j, at=at: e.transpose(
                    bank[:, at:at + 128], Pt[:, POFF[i] + j * 128:POFF[i] + j * 128 + 128], ident[:, :]),
                    [d["norm"], e_id] + list(bf), chan("s_T") if (j == GROUPS[u][-1] and i == 3) else None)
                at += 128
        e1 = copy("scalar", PTt[:, 0, base:base + at], bank[:, 0:at], [ev] + list(tf), chan("s_pthi"))
        e2 = minus("vector", PTt[:, 1, base:base + at], bank[:, 0:at], PTt[:, 0, base:base + at],
                   [e1] + list(tf), chan("s_ptlo"))
        Tr.free[k] = [e2]
        d["pt_ev"].append(e2)
        if u == 2:
            Pb.free[pk] = [ev]

    def av(g):
        d = hd[g]
        P, a = g // 2, g % 2
        Hf = P // 4
        vb, Vt, _, evv = halfV[Hf]
        tk, PTt, _ = d["PT"]
        k, bank, bf = Or.take()
        n = 0
        for j in range(4):
            w = Vt[:, j, P % 4, a * 128:a * 128 + 128]
            for part in range(2):
                n += 1
                sl = slice(OFF[j], OFF[j] + 512 - 128 * j)
                ev = put("tensor", lambda e, j=j, w=w, part=part, sl=sl, n=n: e.matmul(
                    bank[:, 128 * j:512], w, PTt[:, part, sl], start=n == 1, stop=n == 8),
                    list(bf) + [evv] + d["pt_ev"], chan("s_av") if n == 8 else None)
        PTb.free[tk] = [ev]
        if g % 8 == 7:
            Vb.free[vb] = [ev]
        main, rest = (slice(0, 64), slice(64, 128)) if a == 0 else (slice(64, 128), slice(0, 64))
        xk, tm, xf = tmpb.take()
        e1 = put("scalar", lambda e: e.activation(tm[main, :], bank[rest, :], ACT.Copy), [ev] + list(xf),
                 chan("s_ytmp"))
        if a == 0:
            d["Yf"] = Yf.take()
        else:
            d["Yf"] = hd[g - 1]["Yf"]
        yk, Yt, yfree = d["Yf"]
        e2 = put("vector", lambda e: e.tensor_tensor(Yt[main, :], bank[main, :], tm[main, :], ALU.add),
                 [e1] + list(yfree), chan("s_y"))
        Or.free[k] = [e2]
        tmpb.free[xk] = [e2]
        if a == 1:
            ok, Yo, of = Yb.take()
            e3 = copy("gpsimd", Yo[:, 0, :], Yt[:, :], [e2] + list(of), chan("s_yhi"))
            e4 = minus("gpsimd", Yo[:, 1, :], Yt[:, :], Yo[:, 0, :], [e3], chan("s_ylo"))
            Yf.free[yk] = [e4]
            Yslot[P] = (ok, Yo, e4)

    NG = B * H
    bg += ln1(0)
    bg += [vproj(0, t) for t in range(4)]
    bg += [proj(0, "k"), proj(0, "q")]
    need(("q", 0))
    for g in range(NG + 2):
        P, a = g // 2, g % 2
        if g < NG and a == 0:
            b = P // 8
            if P + 1 < NG // 2:
                bg += [proj(P + 1, "k"), proj(P + 1, "q")]
            if P % 8 == 2 and b + 1 < B:
                bg += ln1(b + 1)
            Hf = P // 4 + 1
            if Hf < 2 * B:
                bg.append(vproj(Hf, P % 4))
        if g < NG:
            if g >= 1:
                normalise(g - 1)
            scores(g, 3)
        else:
            if g == NG:
                normalise(g - 1)
        if g >= 2:
            av(g - 2)
            if (g - 2) % 4 == 3:
                bg += [oproj((g - 2) // 4, 0), oproj((g - 2) // 4, 1)]
        if g < NG:
            scores(g, 2)
            scores(g, 1)
        if 1 <= g <= NG:
            transposes(g - 1, 0)
        run_bg(1)
        if g < NG:
            scores(g, 0)
        if 1 <= g <= NG:
            transposes(g - 1, 1)
            transposes(g - 1, 2)
        run_bg(1 + (len(bg) > 4))
    run_bg(len(bg))
    attn_done = list(e_st1.values()) + [hd[NG - 1]["norm"]]
    pe_last = e_xacc[B - 1, 1]
    cx.close()

    phase = [(chan(n), chan(n).n) for n in sems if sems[n].n]

    cx = ExitStack()
    w1 = sbf(root, "w1", [128, 2, 2, 1024], f32r)
    w2 = sbf(root, "w2", [128, 2, 2, 1024], f32r)
    s1c = sbf(root, "s1c", [128, 4, 8])
    XW = [sbf(cx, f"XW{i}", [128, 2, 2, 256], f32r) for i in range(3)]
    ctf = sbf(cx, "ctf", [128, 2, 512])
    ctr = sbf(cx, "ctr", [128, 2, 2, 512], f32r)
    kf = sbf(cx, "kf", [128, 2, 512])
    kT = sbf(cx, "kT", [128, 2, 2, 512], f32r)
    vf_ = sbf(cx, "vf", [128, 4, 256])
    vT = sbf(cx, "vT", [128, 4, 2, 256], f32r)
    bqk = sbf(cx, "bqk", [128, 2, 2])
    bvb = sbf(cx, "bvb", [128, 256])
    mi = sbf(cx, "mi", [128, 256], i32)
    m01 = sbf(cx, "m01", [128, 256])
    mneg = sbf(cx, "mneg", [128, 256])
    xs = Ring([sbf(cx, f"xs{i}", [128, NT, 256]) for i in range(3)])
    xns = Ring([sbf(cx, f"xns{i}", [128, NT, 256]) for i in range(2)])
    XTs = Ring([sbf(cx, f"XTs{i}", [128, 2, 2, 512], f32r) for i in range(2)])
    qf = Ring([sbf(cx, f"qf{i}", [128, 2, 512]) for i in range(1)])
    qT = Ring([sbf(cx, f"qT{i}", [128, 2, 2, 512], f32r) for i in range(2)])
    sf = Ring([sbf(cx, f"sf{i}", [128, 4, 64]) for i in range(2)])
    pf2 = [sbf(cx, f"pf{i}", [128, 4, 128]) for i in range(2)]
    pT = Ring([sbf(cx, f"pT{i}", [128, 2, 512], f32r) for i in range(2)])
    sm2 = Ring([sbf(cx, f"sm{i}", [128, NT, 9]) for i in range(2)])
    st2 = Ring([sbf(cx, f"st{i}", [128, 12]) for i in range(2)])
    stage = Ring([sbf(cx, f"stg{i}", [128, 1024]) for i in range(3)])

    for e in Q.q:
        Q.wait(e, phase)

    G8 = Ring(psum)

    e_xw = []
    for i, n in enumerate(("xwk", "xwv", "xwq")):
        e_xw.append(split_weight(stage, flat(XW[i], 0), flat(XW[i], 1), A[n], 512))
    e_small = [dma(bqk[:, :, :], A["bqk"], "s_bqk"), dma(bvb[:, :], A["bv"].broadcast_to([128, 256]), "s_bvb"),
               dma(mi[:, :], A["mask"], "s_mask"), dma(s1c[:, :, :], A["sc"], "s_sc")]
    ect = dma(ctf[:, :, :], A["ctxT"], "s_ctx")
    e1 = copy("scalar", ctr[:, 0, :, :], ctf[:, :, :], [ect], chan("s_cthi"))
    e_ct = minus("vector", ctr[:, 1, :, :], ctf[:, :, :], ctr[:, 0, :, :], [e1], chan("s_ctlo"))
    e1 = put("vector", lambda e: e.tensor_scalar(m01[:, :], mi[:, :], 0.0, None, ALU.not_equal), [e_small[2]],
             chan("s_m"))
    e_m = put("vector", lambda e: e.tensor_scalar(mneg[:, :], m01[:, :], 1.0, 1e9, ALU.subtract, ALU.mult), [e1],
              chan("s_m"))
    ek = []
    for m in range(2):
        k, bank, bf = G8.take()
        for c in range(2):
            ev = mm3(bank[:, :], XW[0][:, 0, c, m * 128:m * 128 + 128], XW[0][:, 1, c, m * 128:m * 128 + 128],
                     ctr[:, 0, c, :], ctr[:, 1, c, :], c == 0, c == 1, e_xw[0] + [e_ct],
                     chan("s_xk") if c else None)
        e1 = put("vector", lambda e, m=m, bank=bank: e.tensor_scalar(kf[:, m, :], bank[:, :], bqk[:, 1, m:m + 1], None,
                 ALU.add), [ev, e_small[0]], chan("s_xkf"))
        G8.free[k] = [e1]
        e2 = copy("scalar", kT[:, 0, m, :], kf[:, m, :], [e1], chan("s_xkhi"))
        e3 = minus("vector", kT[:, 1, m, :], kf[:, m, :], kT[:, 0, m, :], [e2], chan("s_xklo"))
        ek.append(e3)
    ev_ = []
    for w in range(4):
        k, bank, bf = G8.take()
        ws = slice(w * 128, w * 128 + 128)
        for c in range(2):
            ev = mm3(bank[:, 0:256], ctr[:, 0, c, ws], ctr[:, 1, c, ws], XW[1][:, 0, c, :], XW[1][:, 1, c, :],
                     c == 0, c == 1, e_xw[1] + [e_ct], chan("s_xv") if c else None)
        e1 = put("vector", lambda e, w=w, bank=bank: e.tensor_tensor(vf_[:, w, :], bank[:, 0:256], bvb[:, :], ALU.add),
                 [ev, e_small[1]], chan("s_xvf"))
        G8.free[k] = [e1]
        e2 = copy("scalar", vT[:, w, 0, :], vf_[:, w, :], [e1], chan("s_xvhi"))
        ev_.append(minus("vector", vT[:, w, 1, :], vf_[:, w, :], vT[:, w, 0, :], [e2], chan("s_xvlo")))
    for i in range(2):
        e_pz = put("gpsimd", lambda e, i=i: e.memset(pf2[i][:, :, :], 0.0), (), s_c)
    pf_free = [[e_pz], [e_pz]]
    X = {}
    e_x2 = {}

    def xa_load(b):
        d = X[b] = {}
        d["x"] = xs.take()
        d["e_x"] = dma(d["x"][1][:, :, :], x1_v[b], f"s_xs{d['x'][0]}", d["x"][2])

    def xa_ln(b):
        d = X[b]
        d["xn"] = xns.take()
        d["sm"] = sm2.take()
        d["e_xn"] = layernorm("l2", d["x"][1], d["xn"][1], d["sm"][1], [d["e_x"]], d["xn"][2] + d["sm"][2])
        sm2.free[d["sm"][0]] = [d["e_xn"]]

    def xa_q(b):
        d = X[b]
        d["XT"] = XTs.take()
        es = [transpose_split(d["xn"][1], d["e_xn"], d["XT"][1], d["XT"][2], G8, j) for j in range(2)]
        xns.free[d["xn"][0]] = es
        d["e_XT"] = es
        d["qf"] = qf.take()
        d["qT"] = qT.take()
        Xt = d["XT"][1]
        d["e_q"] = []
        for m in range(2):
            k, bank, bf = G8.take()
            ms = slice(m * 128, m * 128 + 128)
            for c in range(2):
                ev = mm3(bank[:, :], XW[2][:, 0, c, ms], XW[2][:, 1, c, ms], Xt[:, 0, c, :], Xt[:, 1, c, :],
                         c == 0, c == 1, list(bf) + es + e_xw[2], chan("s_xq") if c else None)
            qt, qtt = d["qf"][1], d["qT"][1]
            e1 = put("vector", lambda e, m=m, bank=bank, qt=qt: e.tensor_scalar(
                qt[:, m, :], bank[:, :], bqk[:, 0, m:m + 1], None, ALU.add), [ev] + d["qf"][2], chan("s_xqf"))
            G8.free[k] = [e1]
            e2 = copy("scalar", qtt[:, 0, m, :], qt[:, m, :], [e1] + d["qT"][2], chan("s_xqhi"))
            e3 = minus("gpsimd", qtt[:, 1, m, :], qt[:, m, :], qtt[:, 0, m, :], [e2] + d["qT"][2], chan("s_xqlo"))
            d["e_q"].append(e3)
        qf.free[d["qf"][0]] = [e3]
        XTs.free[d["XT"][0]] = [ev]

    def xa_s(b):
        d = X[b]
        k, bank, bf = G8.take()
        qtt = d["qT"][1]
        ks = slice(b * 64, b * 64 + 64)
        for t in range(4):
            ts = slice(t * 128, t * 128 + 128)
            for c in range(2):
                ev = mm3(bank[:, t * 64:t * 64 + 64], qtt[:, 0, c, ts], qtt[:, 1, c, ts], kT[:, 0, c, ks],
                         kT[:, 1, c, ks], c == 0, c == 1, list(bf) + d["e_q"] + ek,
                         chan("s_xS") if (t == 3 and c == 1) else None)
        qT.free[d["qT"][0]] = [ev]
        sk, st_, sfree = sf.take()
        s4 = st_[:, :, :].rearrange("p t k -> p (t k)")
        e1 = put("vector", lambda e: e.tensor_tensor(s4, bank[:, 0:256], m01[:, :], ALU.mult), [ev, e_m] + list(sfree),
                 chan("s_xs1"))
        G8.free[k] = [e1]
        e1 = put("vector", lambda e: e.tensor_tensor(s4, s4, mneg[:, :], ALU.add), [e1], chan("s_xs1"))
        tk, stt, stf = st2.take()
        e1 = put("vector", lambda e: e.tensor_reduce(stt[:, 0:4], st_[:, :, :], AX.X, ALU.max, negate=True),
                 [e1] + list(stf), chan("s_xs1"))
        pt = pf2[b % 2]
        o = 64 * (b % 2)
        for t in range(4):
            e2 = put("scalar", lambda e, t=t: e.activation(pt[:, t, o:o + 64], st_[:, t, :], ACT.Exp,
                     bias=stt[:, t:t + 1], scale=1.0, accum_out=stt[:, 4 + t:5 + t]), [e1] + pf_free[b % 2],
                     chan("s_xe"))
        sf.free[sk] = [e2]
        e3 = put("vector", lambda e: e.reciprocal(stt[:, 8:12], stt[:, 4:8]), [e2], chan("s_xr"))
        for t in range(4):
            e4 = put("gpsimd", lambda e, t=t: e.tensor_scalar(pt[:, t, o:o + 64], pt[:, t, o:o + 64],
                     stt[:, 8 + t:9 + t], 1.0, ALU.mult, ALU.mult), [e3], chan("s_xn"))
        st2.free[tk] = [e4]
        d["e_p"] = e4

    def xa_o(b):
        d = X[b]
        pt = pf2[b % 2]
        k, bank, bf = G8.take()
        for t in range(4):
            ev = put("tensor", lambda e, t=t, bank=bank: e.transpose(bank[:, t * 128:t * 128 + 128], pt[:, t, :],
                     ident[:, :]),
                     list(bf) + [d["e_p"]], chan("s_xpT") if t == 3 else None)
        pf_free[b % 2] = [ev]
        pk, ptt, pfr = pT.take()
        e1 = copy("scalar", ptt[:, 0, :], bank[:, :], [ev] + list(pfr), chan("s_xphi"))
        e2 = minus("vector", ptt[:, 1, :], bank[:, :], ptt[:, 0, :], [e1], chan("s_xplo"))
        G8.free[k] = [e2]
        w = b // 2
        xk, xt, _ = d["x"]
        es = []
        for tt in range(2):
            k, bank, bf = G8.take()
            for t in range(2):
                ts = slice((2 * tt + t) * 128, (2 * tt + t) * 128 + 128)
                ev = mm3(bank[:, t * 256:t * 256 + 256], ptt[:, 0, ts], ptt[:, 1, ts], vT[:, w, 0, :], vT[:, w, 1, :],
                         True, True, list(bf) + [e2, ev_[w]], chan("s_xo") if t else None)
            xv = xt[:, 2 * tt:2 * tt + 2, :].rearrange("p t c -> p (t c)")
            e3 = put("vector", lambda e, bank=bank, xv=xv: e.tensor_tensor(xv, xv, bank[:, :], ALU.add),
                     [ev, d["e_xn"]], chan("s_xacc2"))
            G8.free[k] = [e3]
            es.append(e3)
        pT.free[pk] = [ev]
        e_x2[b] = dma(x2_v[b], xt[:, :, :], f"s_x2st{xk}", es)
        xs.free[xk] = [e_x2[b]]

    xa_load(0)
    xa_load(1)
    xa_ln(0)
    xa_q(0)
    for b in range(B):
        if b + 2 < B:
            xa_load(b + 2)
        if b + 1 < B:
            xa_ln(b + 1)
        xa_s(b)
        if b + 1 < B:
            xa_q(b + 1)
        xa_o(b)
    e_w1 = split_weight(stage, flat(w1, 0), flat(w1, 1), A["w1"], 2048, eng=("gpsimd", "gpsimd"))
    e_w2 = split_weight(stage, flat(w2, 0), flat(w2, 1), A["w2"], 2048, eng=("gpsimd", "gpsimd"))
    cx.close()
    phase = [(chan(n), chan(n).n) for n in sems if sems[n].n]

    cx = ExitStack()
    hw = sbf(root, "hw", [128, 2, 8, 1024], f32r)
    w3 = sbf(root, "w3", [128, 2, 8, 256], f32r)
    Hb = sbf(root, "Hb", [128, 2, 8, 512], f32r)
    stage = Ring([sbf(root, f"stgf{i}", [128, 1024]) for i in range(2)])
    s3b = sbf(root, "s3b", [128, 256])
    xs = Ring([sbf(cx, f"xf{i}", [128, NT, 256]) for i in range(2)])
    xns = Ring([sbf(cx, f"xnf{i}", [128, NT, 256]) for i in range(1)])
    XTs = Ring([sbf(cx, f"XTf{i}", [128, 2, 2, 512], f32r) for i in range(2)])
    sm2 = Ring([sbf(cx, f"smf{i}", [128, NT, 9]) for i in range(1)])
    gt = Ring([sbf(cx, f"gt{i}", [128, 512]) for i in range(2)])
    ht = Ring([sbf(cx, f"ht{i}", [128, 512]) for i in range(2)])
    go_ = Ring([sbf(cx, f"go{i}", [128, 512]) for i in range(2)])

    for e in Q.q:
        Q.wait(e, phase)
    e_s3 = dma(s3b[:, :], A["s3"].broadcast_to([128, 256]), "s_s3")
    G8 = Ring(psum)
    hwf = lambda i, m: hw[:, i, m, :]
    e_h1 = [split_weight(stage, hwf(0, m), hwf(1, m), A["h1"][m], 1024) for m in range(8)]
    F = {}

    def f_load(b):
        d = F[b] = {}
        d["x"] = xs.take()
        d["e_x"] = dma(d["x"][1][:, :, :], x2_v[b], f"s_xf{d['x'][0]}", d["x"][2] + [e_x2[b]])

    def f_ln(b):
        d = F[b]
        d["xn"] = xns.take()
        d["sm"] = sm2.take()
        d["e_xn"] = layernorm("l3", d["x"][1], d["xn"][1], d["sm"][1], [d["e_x"]], d["xn"][2] + d["sm"][2])
        sm2.free[d["sm"][0]] = [d["e_xn"]]
        xs.free[d["x"][0]] = [d["e_xn"]]

    def f_xt(b):
        d = F[b]
        d["XT"] = XTs.take()
        d["e_XT"] = [transpose_split(d["xn"][1], d["e_xn"], d["XT"][1], d["XT"][2], G8, j) for j in range(2)]
        xns.free[d["xn"][0]] = d["e_XT"]

    e_H = [None] * 8
    H_free = [[] for _ in range(8)]

    def f_w(b, m):
        d = F[b]
        Xt = d["XT"][1]
        ms = slice(m * 128, m * 128 + 128)
        res = []
        for W, ew in ((w1, e_w1), (w2, e_w2)):
            k, bank, bf = G8.take()
            for c in range(2):
                ev = mm3(bank[:, :], W[:, 0, c, ms], W[:, 1, c, ms], Xt[:, 0, c, :], Xt[:, 1, c, :], c == 0, c == 1,
                         list(bf) + d["e_XT"] + ew, chan("s_gu") if c else None)
            res.append((k, bank, ev))
        (k1, bk1, ev1), (k2, bk2, ev2) = res
        if m == 7:
            XTs.free[d["XT"][0]] = [ev2]
        gk, g_, gf = gt.take()
        e1 = put("scalar", lambda e: e.activation(g_[:, :], bk1[:, :], ACT.Silu, scale=s1c[:, 0, m:m + 1]),
                 [ev1] + list(gf), chan("s_silu"))
        G8.free[k1] = [e1]
        hk, h_, hf = ht.take()
        e2 = put("vector", lambda e: e.scalar_tensor_tensor(h_[:, :], bk2[:, :], s1c[:, 1, m:m + 1], g_[:, :],
                 ALU.mult, ALU.mult), [ev2, e1] + list(hf), chan("s_h"))
        G8.free[k2] = [e2]
        gt.free[gk] = [e2]
        e3 = copy("scalar", Hb[:, 0, m, :], h_[:, :], [e2] + H_free[m], chan("s_hhi"))
        e4 = minus("vector", Hb[:, 1, m, :], h_[:, :], Hb[:, 0, m, :], [e3] + H_free[m], chan("s_hlo"))
        ht.free[hk] = [e4]
        e_H[m] = e4

    def hidden(m, e_h, name):
        k, bank, bf = G8.take()
        for c in range(8):
            cs = slice(c * 128, c * 128 + 128)
            ev = mm3(bank[:, :], hw[:, 0, m, cs], hw[:, 1, m, cs], Hb[:, 0, c, :], Hb[:, 1, c, :], c == 0, c == 7,
                     list(bf) + [e_H[c]] + e_h[m], chan("s_hid") if c == 7 else None)
            if m == 7:
                H_free[c] = [ev]
        return k, bank, ev

    e_hst = {}

    def f_h(b, m):
        k, bank, ev = hidden(m, e_h1, "h1")
        if m == 7:
            for c in range(8):
                H_free[c] = [ev]
        ok, o_, of = go_.take()
        e1 = put("scalar", lambda e: e.activation(o_[:, :], bank[:, :], ACT.Gelu, scale=s1c[:, 2, m:m + 1]),
                 [ev] + list(of), chan("s_gelu"))
        G8.free[k] = [e1]
        e_hst[b, m] = dma(h_d[b, m], o_[:, :], f"s_hst{ok}", [e1])
        go_.free[ok] = [e_hst[b, m]]
        return ev

    f_load(0)
    f_ln(0)
    f_xt(0)
    f_load(1)
    e_hw_last = [None] * 8
    for b in range(B):
        for m in range(8):
            f_w(b, m)
        if b + 1 < B:
            f_ln(b + 1)
            if b + 2 < B:
                f_load(b + 2)
        for m in range(8):
            e_hw_last[m] = f_h(b, m)
            if m == 4 and b + 1 < B:
                f_xt(b + 1)
    e_h2 = [split_weight(stage, hwf(0, m), hwf(1, m), A["h2"][m], 1024, waits=[e_hw_last[m]],
            eng=("gpsimd", "vector")) for m in range(8)]
    e_w3 = split_weight(stage, flat(w3, 0), flat(w3, 1), A["w3"], 2048, eng=("gpsimd", "vector"))
    phase = [(chan(n), chan(n).n) for n in ("s_hst0", "s_hst1", "s_gelu", "s_hlo", "s_hid", "s_gu")]
    cx.close()

    cx = ExitStack()
    Gb = [w[:, :, :, :].rearrange("p a k f -> p (a k f)").rearrange("p (c n) -> p c n", c=8) for w in (w1, w2)]
    hl = Ring([sbf(cx, f"hl{i}", [128, 512]) for i in range(4)])
    xs = Ring([sbf(cx, f"xg{i}", [128, NT, 256]) for i in range(2)])
    gt = Ring([sbf(cx, f"gg{i}", [128, 512]) for i in range(2)])
    ot = Ring([sbf(cx, f"ot{i}", [128, 512]) for i in range(2)])
    for e in Q.q:
        Q.wait(e, phase)
    e_G = [None] * 8
    G_free = [[] for _ in range(8)]

    def g_load(b, m):
        k, t, f = hl.take()
        e0 = dma(t[:, :], h_d[b, m], f"s_hl{k}", list(f) + [e_hst[b, m]])
        e1 = copy("gpsimd", Hb[:, 0, m, :], t[:, :], [e0] + H_free[m], chan("s_h2hi"))
        e2 = minus("vector", Hb[:, 1, m, :], t[:, :], Hb[:, 0, m, :], [e1] + H_free[m], chan("s_h2lo"))
        hl.free[k] = [e2]
        e_H[m] = e2

    def g_h(m):
        k, bank, ev = hidden(m, e_h2, "h2")
        gk, g_, gf = gt.take()
        e1 = put("scalar", lambda e: e.activation(g_[:, :], bank[:, :], ACT.Gelu, scale=s1c[:, 3, m:m + 1]),
                 [ev] + list(gf), chan("s_gelu2"))
        G8.free[k] = [e1]
        e2 = copy("gpsimd", Gb[0][:, m, :], g_[:, :], [e1] + G_free[m], chan("s_ghi"))
        e3 = minus("vector", Gb[1][:, m, :], g_[:, :], Gb[0][:, m, :], [e2] + G_free[m], chan("s_glo"))
        gt.free[gk] = [e3]
        e_G[m] = e3

    xg = {}

    def g_out(b, tt):
        k, bank, bf = G8.take()
        for t in range(2):
            ts = slice((2 * tt + t) * 128, (2 * tt + t) * 128 + 128)
            for c in range(8):
                ev = mm3(bank[:, t * 256:t * 256 + 256], Gb[0][:, c, ts], Gb[1][:, c, ts], w3[:, 0, c, :],
                         w3[:, 1, c, :], c == 0, c == 7, list(bf) + [e_G[c]] + e_w3,
                         chan("s_out") if (t == 1 and c == 7) else None)
        if tt == 1:
            for c in range(8):
                G_free[c] = [ev]
        ok, o_, of = ot.take()
        es = []
        for t in range(2):
            e1 = put("vector", lambda e, t=t: e.tensor_tensor(o_[:, t * 256:t * 256 + 256],
                     bank[:, t * 256:t * 256 + 256], s3b[:, :], ALU.mult), [ev, e_s3] + list(of), chan("s_fs"))
        G8.free[k] = [e1]
        xk, xt, _, ex = xg[b]
        xv = xt[:, 2 * tt:2 * tt + 2, :].rearrange("p t c -> p (t c)")
        e2 = put("vector", lambda e: e.tensor_tensor(o_[:, :], o_[:, :], xv, ALU.add), [e1, ex], chan("s_fs"))
        e3 = dma(out_v[b][:, 2 * tt:2 * tt + 2, :].rearrange("p t c -> p t c"),
                 o_[:, :].rearrange("p (t c) -> p t c", t=2), f"s_final{ok}", [e2])
        ot.free[ok] = [e3]
        if tt == 1:
            xs.free[xk] = [e2]

    for m in range(8):
        g_load(0, m)
    for b in range(B):
        k, t, f = xs.take()
        xg[b] = (k, t, f, dma(t[:, :, :], x2_v[b], f"s_xg{k}", list(f) + [e_x2[b]]))
        for m in range(8):
            g_h(m)
        if b:
            pass
        if b + 1 < B:
            for m in range(8):
                g_load(b + 1, m)
        g_out(b, 0)
        g_out(b, 1)
    cx.close()
    Q.wait("sync", [(c, c.n) for n, c in sems.items() if n[:-1] in ("s_final", "s_x1st", "s_x2st", "s_hst")])

    with nc.Block() as block:
        @block.sync
        def _(e):
            for f in Q.q["sync"]:
                f(e)

        @block.gpsimd
        def _(e):
            for f in Q.q["gpsimd"]:
                f(e)

        @block.scalar
        def _(e):
            for f in Q.q["scalar"]:
                f(e)

        @block.vector
        def _(e):
            for f in Q.q["vector"]:
                f(e)

        @block.tensor
        def _(e):
            for f in Q.q["tensor"]:
                f(e)
    root.close()


def kernel(**inputs):
    import numpy as np
    import concourse.bacc as _bacc
    from concourse import mybir as _mybir
    from concourse.bass_utils import run_bass_kernel_spmd as _run

    I = {k: np.asarray(v) for k, v in inputs.items()}

    def kt(w):
        o, i = w.shape
        return w.T.reshape(i // 128, 128, o).transpose(1, 0, 2).reshape(128, -1)

    def mkt(w):
        o, i = w.shape
        return w.T.reshape(i // 128, 128, o // 128, 128).transpose(2, 1, 0, 3).reshape(o // 128, 128, i)

    col = lambda v: v.reshape(-1, 128).T
    a = {
        "x": I["x"],
        "wq": kt(I["L0_attn_w_q"].reshape(1024, 256)),
        "wk": kt(I["L0_attn_w_k"].reshape(1024, 256)),
        "wv": kt(I["L0_attn_w_v"].reshape(1024, 256)),
        "wo": kt(I["L0_attn_w_o"].T),
        "xwq": kt(I["L0_xattn_Wq"]),
        "xwk": kt(I["L0_xattn_Wk"]),
        "xwv": kt(I["L0_xattn_Wv"]),
        "bqk": np.stack([col(I["L0_xattn_bq"]), col(I["L0_xattn_bk"])], 1),
        "bv": I["L0_xattn_bv"].reshape(1, 256),
        "ctxT": I["ctx_1024"].reshape(512, 256).T.reshape(2, 128, 512).transpose(1, 0, 2),
        "mask": I["mask_SxS2_ik1"].reshape(4, 128, 64).transpose(1, 0, 2).reshape(128, 256),
        "w1": kt(I["L0_ffn_w1_w"]),
        "w2": kt(I["L0_ffn_w2_w"]),
        "h1": mkt(I["L0_ffn_h1_w"]),
        "h2": mkt(I["L0_ffn_h2_w"]),
        "w3": kt(I["L0_ffn_w3_w"]),
        "sc": np.stack([col(I[f"L0_ffn_{n}_s"]) for n in ("w1", "w2", "h1", "h2")], 1),
        "s3": I["L0_ffn_w3_s"].reshape(1, 256),
    }
    a = {k: np.ascontiguousarray(v) for k, v in a.items()}
    nc = _bacc.Bacc("TRN2", target_bir_lowering=False, num_devices=1)
    aps = {k: nc.dram_tensor(f"in_{k}", v.shape, _mybir.dt.from_np(v.dtype), kind="ExternalInput").ap()
           for k, v in a.items()}
    out = nc.dram_tensor("out_0", (B, T, C), _mybir.dt.float32, kind="ExternalOutput").ap()
    program(nc, aps, out)
    r = _run(nc, [{f"in_{k}": v for k, v in a.items()}], core_ids=[0])
    return r.results[0]["out_0"]
```

```python
import concourse.bass as bass
from concourse import mybir
from contextlib import ExitStack


class Chan:

    def __init__(self, sem, step=1):
        self.sem, self.step, self.n = sem, step, 0


class Queues:

    def __init__(self):
        self.q = {k: [] for k in ("tensor", "vector", "scalar", "gpsimd", "sync")}
        self.seen = {k: {} for k in self.q}

    def wait(self, eng, events):
        for ev in events:
            if ev is None:
                continue
            ch, n = ev
            if self.seen[eng].get(ch, 0) < n:
                self.seen[eng][ch] = n
                self.q[eng].append(lambda e, ch=ch, n=n: e.wait_ge(ch.sem, n))

    def put(self, eng, fn, waits=(), sig=None):
        self.wait(eng, waits)
        if sig is None:
            self.q[eng].append(fn)
            return None
        sig.n += sig.step
        self.q[eng].append(lambda e: fn(e).then_inc(sig.sem, sig.step))
        return (sig, sig.n)


class Ring:

    def __init__(self, tiles):
        self.tiles, self.free, self.i = tiles, [[] for _ in tiles], -1

    def ready(self):
        return self.free[(self.i + 1) % len(self.tiles)] is not None

    def take(self):
        self.i += 1
        k = self.i % len(self.tiles)
        f, self.free[k] = self.free[k], None
        assert f is not None
        return k, self.tiles[k], f


B, T, C, H = 8, 512, 256, 16
NT = 4
S2 = 64
NEG = -1e30
DX, DN, DL, LAG = 2, 1, 1, 2
ORDER = ("S3", "T0", "AV", "S2", "T1", "S1", "bg", "T2", "S0", "bg")
EPS = 1e-5


def program(nc, A, out):
    RMAX = bass.bass_isa.ReduceOp.max
    f32, f32r, i32 = mybir.dt.float32, mybir.dt.float32r, mybir.dt.int32
    ACT, ALU, AX = mybir.ActivationFunctionType, mybir.AluOpType, mybir.AxisListType
    Q = Queues()
    put = Q.put
    root = ExitStack()
    x1_d = nc.dram_tensor("x1_scratch", (B, T, C), f32, kind="Internal").ap()
    x2_d = nc.dram_tensor("x2_scratch", (B, T, C), f32, kind="Internal").ap()
    h_d = nc.dram_tensor("h_scratch", (B, 8, 128, T), f32, kind="Internal").ap()
    sems = {}

    def chan(name, step=1):
        if name not in sems:
            sems[name] = Chan(root.enter_context(nc.semaphore(name)), step)
        return sems[name]

    def dma(dst, src, name, waits=()):
        return put("sync", lambda e: e.dma_start(dst, src), waits, chan(name, 16))

    psum = [root.enter_context(nc.psum_tensor(f"bank{i}", [128, 512], f32)) for i in range(8)]

    def sbf(cx, name, shape, dt=f32):
        return cx.enter_context(nc.sbuf_tensor(name, shape, dt))

    ident = sbf(root, "ident", [128, 128])
    identr = sbf(root, "identr", [128, 128], f32r)
    s_c = chan("s_const")
    e0 = put("gpsimd", lambda e: e.memset(ident[:, :], 0.0), (), s_c)
    e_id = put("gpsimd", lambda e: e.affine_select(out=ident[:, :], in_=ident[:, :], compare_op=ALU.not_equal,
               fill=1.0, base=0, pattern=[[-1, 128]], channel_multiplier=1), [e0], s_c)
    e_idr = put("scalar", lambda e: e.activation(identr[:, :], ident[:, :], ACT.Copy), [e_id], chan("s_identr"))

    def copy(eng, dst, src, waits, sig, scale=1.0):
        if eng == "scalar":
            return put(eng, lambda e: e.activation(dst, src, ACT.Copy, scale=scale), waits, sig)
        return put(eng, lambda e: e.tensor_scalar(dst, src, scale, 1.0, ALU.mult, ALU.mult), waits, sig)

    def minus(eng, dst, a, b, waits, sig):
        return put(eng, lambda e: e.tensor_tensor(dst, a, b.bitcast(f32), ALU.subtract), waits, sig)

    stage_n = [0]

    def split_weight(ring, dst_hi, dst_lo, src, n, scale=1.0, waits=(), eng=("scalar", "vector"), rest_max=None):
        evs = []
        for a in range(0, n, 1024):
            m = min(1024, n - a)
            k, st, free = ring.take()
            e_ld = dma(st[:, 0:m], src[:, a:a + m], f"s_wld{k}", list(free) + list(waits))
            if scale != 1.0:
                e_ld = put("gpsimd", lambda e, st=st, m=m: e.tensor_scalar(
                    st[:, 0:m], st[:, 0:m], scale, 1.0, ALU.mult, ALU.mult), [e_ld], chan("s_wscale"))
            e_hi = copy(eng[0], dst_hi[:, a:a + m], st[:, 0:m], [e_ld] + list(waits), chan("s_whi_" + eng[0]))
            e_lo = minus(eng[1], dst_lo[:, a:a + m], st[:, 0:m], dst_hi[:, a:a + m], [e_hi],
                         chan("s_wlo_" + eng[1]))
            ring.free[k] = [e_lo]
            evs += [e_lo]
            if rest_max is not None:
                tile, at, _ = rest_max
                c, rest_max[1] = at, at + 1
                rest_max[2] = put("vector", lambda e, c=c, a=a, m=m: e.tensor_reduce(
                    tile[:, c:c + 1], dst_lo[:, a:a + m].bitcast(f32), AX.X, ALU.max, apply_absolute_value=True),
                    [e_lo], chan("s_restmax"))
        return evs

    def rest_flag(rest_max, flag, name):
        tile, n, ev = rest_max
        e1 = put("vector", lambda e: e.tensor_reduce(flag[:, 0:1], tile[:, 0:n], AX.X, ALU.max), [ev],
                 chan("s_restmax"))
        return put("gpsimd", lambda e: e.partition_all_reduce(flag[:, 1:2], flag[:, 0:1], 128, RMAX), [e1],
                   chan(name))

    def mm3(dst, whi, wlo, xhi, xlo, first, last, waits, sig):
        put("tensor", lambda e: e.matmul(dst, whi, xhi, start=first, stop=False), waits)
        put("tensor", lambda e: e.matmul(dst, whi, xlo, start=False, stop=False))
        return put("tensor", lambda e: e.matmul(dst, wlo, xhi, start=False, stop=last), (), sig)

    def layernorm(tag, x, xn, small, waits, free):
        st = small[:, :, 0:6]
        mv = small[:, :, 6:8]
        rs = small[:, :, 8:9]
        s = chan("s_ln")
        for t in range(NT):
            ev = put("vector", lambda e, t=t: e.bn_stats(st[:, t, :], x[:, t, :]), list(waits) + list(free), s)
        for t in range(NT):
            ev = put("vector", lambda e, t=t: e.bn_aggr(mv[:, t, :], st[:, t, :]), [ev], s)
        ev = put("vector", lambda e: e.tensor_scalar(rs, mv[:, :, 1:2], EPS, None, ALU.add), [ev], s)
        ev = put("gpsimd", lambda e: e.tensor_tensor(rs, rs, half[:, :].rearrange("p (t o) -> p t o", o=1), ALU.pow),
                 [ev, e_half], chan("s_rstd"))
        for t in range(NT):
            ev2 = put("vector", lambda e, t=t: e.tensor_scalar(xn[:, t, :], x[:, t, :], mv[:, t, 0:1], rs[:, t, :],
                      ALU.subtract, ALU.mult), [ev], s)
        return ev2

    def transpose_split(xn, e_xn, XT, free, ring, j, later=None, then=None):
        k, bank, bf = ring.take()
        for t in range(NT):
            ev = put("tensor", lambda e, t=t: e.transpose(bank[:, t * 128:t * 128 + 128],
                     xn[:, t, j * 128:j * 128 + 128], ident[:, :]), [e_xn, e_id] + list(bf),
                     chan("s_xnT") if t == NT - 1 else None)
        e_hi = copy("scalar", XT[:, 0, j, :], bank[:, :], [ev] + list(free), chan("s_xhi"))
        def rest():
            e_lo = minus("vector", XT[:, 1, j, :], bank[:, :], XT[:, 0, j, :], [e_hi] + list(free), chan("s_xlo"))
            ring.free[k] = [e_lo]
            if then:
                then(e_lo)
            return e_lo
        return later(1, rest) if later else rest()

    half = sbf(root, "half", [128, NT])
    e_half = put("gpsimd", lambda e: e.memset(half[:, :], -0.5), (), s_c)

    cx = ExitStack()
    cmask = sbf(cx, "cmask", [128, 128])
    cmaskr = sbf(cx, "cmaskr", [128, 128], f32r)
    e0 = put("gpsimd", lambda e: e.memset(cmask[:, :], 0.0), (), s_c)
    e0 = put("gpsimd", lambda e: e.affine_select(out=cmask[:, :], in_=cmask[:, :], compare_op=ALU.is_ge, fill=NEG,
             base=0, pattern=[[-1, 128]], channel_multiplier=1), [e0], s_c)
    e_cm = put("scalar", lambda e: e.activation(cmaskr[:, :], cmask[:, :], ACT.Copy), [e0], chan("s_identr"))
    Wq = sbf(cx, "Wq", [128, 2, 2, 1024], f32r)
    Wk = sbf(cx, "Wk", [128, 2, 2, 1024], f32r)
    Wv = sbf(cx, "Wv", [128, 2, 2, 1024], f32r)
    Wo = sbf(cx, "Wo", [128, 2, 8, 256], f32r)
    XTb = [sbf(cx, f"XT{i}", [128, 2, 2, 512], f32r) for i in range(2)]
    Kb = Ring([sbf(cx, f"K{i}", [128, 2, 512], f32r) for i in range(2)])
    Qb = Ring([sbf(cx, f"Qz{i}", [128, 2, 2, 512], f32r) for i in range(2)])
    Vb = Ring([sbf(cx, f"V{i}", [128, NT, 4, 256], f32r) for i in range(2)])
    Pb = Ring([sbf(cx, f"P{i}", [128, 1280]) for i in range(2)])
    PTb = Ring([sbf(cx, f"PT{i}", [128, 2, 1280], f32r) for i in range(2)])
    Yb = Ring([sbf(cx, f"Y{i}", [128, 2, 512], f32r) for i in range(4)])
    Yf = Ring([sbf(cx, "Yf0", [128, 512])])
    tmpb = Ring([sbf(cx, "ytmp", [128, 512])])
    xb = [sbf(cx, f"x{i}", [128, NT, 256]) for i in range(2)]
    xn = sbf(cx, "xn", [128, NT, 256])
    small = sbf(cx, "lnsmall", [128, NT, 9])
    stats = [sbf(cx, f"stats{i}", [128, 12]) for i in range(4)]
    stage = Ring([Pb.tiles[0][:, 0:1024], Pb.tiles[1][:, 0:1024], xb[1][:, :, :].rearrange("p t c -> p (t c)")])

    x_in = A["x"].rearrange("b (t p) c -> b p t c", p=128)
    x1_v = x1_d.rearrange("b (t p) c -> b p t c", p=128)
    x2_v = x2_d.rearrange("b (t p) c -> b p t c", p=128)
    out_v = out.rearrange("b (t p) c -> b p t c", p=128)

    Sr = Ring([psum[i] for i in (0, 1, 2)])
    Tr = Ring([psum[i] for i in (3, 4)])
    Or = Ring([psum[5]])
    Gr = Ring([psum[i] for i in (6, 7)])

    e_x = {0: dma(xb[0][:, :, :], x_in[0], "s_xld0")}
    flat = lambda w, i: w[:, i, :, :].rearrange("p k f -> p (k f)")
    e_wq = split_weight(stage, flat(Wq, 0), flat(Wq, 1), A["wq"], 2048, scale=0.125)
    e_wk = split_weight(stage, flat(Wk, 0), flat(Wk, 1), A["wk"], 2048)
    e_wv = split_weight(stage, flat(Wv, 0), flat(Wv, 1), A["wv"], 2048)
    e_wo = split_weight(stage, flat(Wo, 0), flat(Wo, 1), A["wo"], 2048)
    for i in range(2):
        Pb.free[i] = list(stage.free[i])
    e_x1free = list(stage.free[2])

    for i, q in enumerate(Qb.tiles):
        for a, (lo_p, hi_p) in enumerate(((64, 128), (0, 64))):
            for k in range(2):
                ev = put("vector", lambda e, q=q, a=a, k=k, lo_p=lo_p, hi_p=hi_p: e.memset(
                    q[lo_p:hi_p, a, k, :].bitcast(f32), 0.0), (), chan("s_qzero"))
    e_qz = ev

    slot, due, bg, done = [0], [], [], set()

    def defer(n, fn):
        due.append((slot[0] + n, fn))

    def tick():
        slot[0] += 1
        now = [d for d in due if d[0] <= slot[0]]
        due[:] = [d for d in due if d[0] > slot[0]]
        for _, fn in now:
            fn()

    def until(cond):
        while not cond():
            assert due
            tick()

    def run_bg(n):
        for _ in range(n):
            if bg:
                tag, fn = bg.pop(0)
                fn()
                done.add(tag)
                tick()

    def need(tag):
        while tag not in done:
            assert bg, tag
            run_bg(1)

    e_XT, XT_free, e_xacc = {}, [[], []], {}
    pairQ, pairK, halfV = {}, {}, {}

    def ln1(b):
        def load():
            if b not in e_x:
                e_x[b] = dma(xb[b % 2][:, :, :], x_in[b], f"s_xld{b % 2}",
                             e_x1free if b == 1 else [e_st1[b - 2]])
        def norm():
            load()
            if b:
                until(lambda: len(e_XT[b - 1]) == 2)
            e_xn[b] = layernorm("l1", xb[b % 2], xn, small, [e_x[b]], [e_XT[b - 1][1]] if b else [])
        def tr(j):
            until(lambda: Gr.ready())
            transpose_split(xn, e_xn[b], XTb[b % 2], XT_free[b % 2], Gr, j, later=defer,
                            then=e_XT.setdefault(b, []).append)
        return [(("ln", b), norm), (("xt0", b), lambda: tr(0)), (("xt", b), lambda: tr(1))]
    e_xn, e_st1 = {}, {}

    def proj(P, which):
        b, p = P // 8, P % 8
        def go():
            X = XTb[b % 2]
            until(lambda: len(e_XT.get(b, ())) == 2 and Gr.ready())
            W, ew = (Wq, e_wq) if which == "q" else (Wk, e_wk)
            k, bank, bf = Gr.take()
            fs = slice(p * 128, p * 128 + 128)
            for c in range(2):
                ev = mm3(bank[:, :], W[:, 0, c, fs], W[:, 1, c, fs], X[:, 0, c, :], X[:, 1, c, :],
                         c == 0, c == 1, list(bf) + e_XT[b] + ew, chan("s_qk") if c == 1 else None)
            if which == "k":
                kb, Kt, kf = Kb.take()
                e1 = copy("scalar", Kt[:, 0, :], bank[:, :], [ev] + list(kf), chan("s_qkhi"))

                def rest():
                    e2 = minus("vector", Kt[:, 1, :], bank[:, :], Kt[:, 0, :], [e1], chan("s_qklo"))
                    pairK[P] = (kb, Kt, e2)
                    Gr.free[k] = [e2]
            else:
                qb, Qt, qf = Qb.take()
                for a in range(2):
                    r = slice(64 * a, 64 * a + 64)
                    e1 = copy("scalar", Qt[r, a, 0, :], bank[r, :], [ev, e_qz] + list(qf), chan("s_qkhi"))

                def rest():
                    for a in range(2):
                        r = slice(64 * a, 64 * a + 64)
                        e2 = minus("vector", Qt[r, a, 1, :], bank[r, :], Qt[r, a, 0, :], [e1, e_qz] + list(qf),
                                   chan("s_qklo"))
                    pairQ[P] = (qb, Qt, e2)
                    Gr.free[k] = [e2]
            defer(1, rest)
            if P % 8 == 7 and which == "q":
                XT_free[b % 2] = [ev]
        return ((which, P), go)

    def vproj(Hf, t):
        b, hh = Hf // 2, Hf % 2
        def go():
            until(lambda: len(e_XT.get(b, ())) == 2 and Gr.ready() and Vb.ready() | (t > 0))
            if t == 0:
                halfV[Hf] = [*Vb.take(), None]
            kb, Vt, vf, _ = halfV[Hf]
            X = XTb[b % 2]
            k, bank, bf = Gr.take()
            ts = slice(t * 128, t * 128 + 128)
            fs = slice(hh * 512, hh * 512 + 512)
            for c in range(2):
                ev = mm3(bank[:, :], X[:, 0, c, ts], X[:, 1, c, ts], Wv[:, 0, c, fs], Wv[:, 1, c, fs],
                         c == 0, c == 1, list(bf) + e_XT[b] + e_wv, chan("s_v") if c == 1 else None)
            src = bank[:, :].rearrange("p (q a d) -> p q a d", q=4, a=2)
            v4 = Vt[:, t, :, :].rearrange("p q (s d) -> p q s d", d=64)
            e1 = copy("scalar", v4[:, :, 0:4:3, :], src, [ev] + list(vf), chan("s_vhi"))

            def rest():
                e2 = minus("vector", v4[:, :, 1:3, :], src, v4[:, :, 0:4:3, :], [e1] + list(vf), chan("s_vlo"))
                Gr.free[k] = [e2]
                halfV[Hf][3] = e2
            defer(1, rest)
        return (("v", Hf, t), go)

    Yslot = {}

    def oproj(Qr, tt):
        b = Qr // 4
        def go():
            until(lambda: 2 * Qr + 1 in Yslot and Gr.ready())
            k, bank, bf = Gr.take()
            for t in (2 * tt, 2 * tt + 1):
                o = bank[:, (t % 2) * 256:(t % 2) * 256 + 256]
                ts = slice(t * 128, t * 128 + 128)
                for i in range(2):
                    P = 2 * Qr + i
                    yk, Yt, ey = Yslot[P]
                    ev = mm3(o, Yt[:, 0, ts], Yt[:, 1, ts], Wo[:, 0, P % 8, :], Wo[:, 1, P % 8, :],
                             i == 0, i == 1, list(bf) + [ey] + e_wo, chan("s_o") if i == 1 else None)
            if tt == 1:
                for i in range(2):
                    Yb.free[Yslot[2 * Qr + i][0]] = [ev]
            xt = xb[b % 2][:, 2 * tt:2 * tt + 2, :].rearrange("p t c -> p (t c)")
            e2 = put("vector", lambda e: e.tensor_tensor(xt, xt, bank[:, :], ALU.add), [ev, e_xn[b]]
                     + ([e_xacc[b, tt]] if (b, tt) in e_xacc else []), chan("s_xacc"))
            Gr.free[k] = [e2]
            e_xacc[b, tt] = e2
            if Qr % 4 == 3 and tt == 1:
                e_st1[b] = dma(x1_v[b], xb[b % 2][:, :, :], f"s_x1st{b % 2}", [e2])
        return (("o", Qr, tt), go)

    OFF = {0: 0, 1: 512, 3: 896, 2: 1024}
    POFF = {3: 0, 2: 512, 1: 896, 0: 1152}
    hd = {}

    def scores(g, i):
        P, a = g // 2, g % 2
        if i == 3:
            need(("q", P)), need(("k", P))
            until(lambda: P in pairQ and P in pairK and Pb.ready())
            pk, Pt, pf = Pb.take()
            hd[g] = dict(P=(pk, Pt, pf), exp={})
        d = hd[g]
        qb, Qt, eq = pairQ[P]
        kb, Kt, ek = pairK[P]
        until(Sr.ready)
        k, bank, bf = Sr.take()
        n = 128 * (i + 1)
        qs = slice(i * 128, i * 128 + 128)
        mm3(bank[:, 0:n], Qt[:, a, 0, qs], Qt[:, a, 1, qs], Kt[:, 0, 0:n], Kt[:, 1, 0:n], True, False,
            list(bf) + [eq, ek], None)
        ev = put("tensor", lambda e: e.matmul(bank[:, n - 128:n], identr[:, :], cmaskr[:, :], start=False,
                 stop=True), [e_idr, e_cm], chan("s_S"))
        if a == 1 and i == 0:
            Qb.free[qb] = [ev]
            Kb.free[kb] = [ev]
        st = stats[g % 4]
        e1 = put("vector", lambda e: e.tensor_reduce(st[:, i:i + 1], bank[:, 0:n], AX.X, ALU.max, negate=True),
                 [ev] + ([hd[g - 4]["norm"][0]] if g >= 4 else []), chan("s_max"))
        _, Pt, pf = d["P"]

        def rest():
            e2 = put("scalar", lambda e: e.activation(Pt[:, POFF[i]:POFF[i] + n], bank[:, 0:n], ACT.Exp,
                     bias=st[:, i:i + 1], scale=1.0, accum_out=st[:, 4 + i:5 + i]), [e1] + list(pf), chan("s_exp"))
            Sr.free[k] = [e2]
            d["exp"][i] = e2
            if i in (2, 0):
                defer(DN, lambda: normalise(g, i))
        defer(DX, rest)

    def normalise(g, i0):
        d = hd[g]
        st = stats[g % 4]
        er = put("vector", lambda e: e.reciprocal(st[:, 8 + i0:10 + i0], st[:, 4 + i0:6 + i0]), [d["exp"][i0]],
                 chan("s_recip"))
        Pt = d["P"][1]
        for i in (i0 + 1, i0):
            n = 128 * (i + 1)
            ev = put("gpsimd", lambda e, i=i, n=n: e.tensor_scalar(
                Pt[:, POFF[i]:POFF[i] + n], Pt[:, POFF[i]:POFF[i] + n], st[:, 8 + i:9 + i], 1.0,
                ALU.mult, ALU.mult), [er], chan("s_norm"))
            d.setdefault("norm", {})[i] = ev

    GROUPS = [[2], [1, 3], [0]]

    def transposes(g, u):
        d = hd[g]
        pk, Pt, _ = d["P"]
        until(lambda: GROUPS[u][0] in d["norm"] and Tr.ready() and (u > 0 or PTb.ready()))
        if u == 0:
            d["PT"] = PTb.take()
            d["pt_ev"] = {}
        tk, PTt, tf = d["PT"]
        k, bank, bf = Tr.take()
        base = OFF[GROUPS[u][0]]
        at = 0
        for j in GROUPS[u]:
            for i in range(j, 4):
                ev = put("tensor", lambda e, i=i, j=j, at=at: e.transpose(
                    bank[:, at:at + 128], Pt[:, POFF[i] + j * 128:POFF[i] + j * 128 + 128], ident[:, :]),
                    [d["norm"][i], e_id] + list(bf), chan("s_T") if (j == GROUPS[u][-1] and i == 3) else None)
                at += 128
        e1 = copy("scalar", PTt[:, 0, base:base + at], bank[:, 0:at], [ev] + list(tf), chan("s_pthi"))

        def rest():
            e2 = minus("vector", PTt[:, 1, base:base + at], bank[:, 0:at], PTt[:, 0, base:base + at],
                       [e1] + list(tf), chan("s_ptlo"))
            Tr.free[k] = [e2]
            for j in GROUPS[u]:
                d["pt_ev"][j] = e2
        defer(DL, rest)
        if u == 2:
            Pb.free[pk] = [ev]

    def av(g):
        d = hd[g]
        P, a = g // 2, g % 2
        Hf = P // 4
        vb, Vt, _, evv = halfV[Hf]
        tk, PTt, _ = d["PT"]
        until(lambda: len(d["pt_ev"]) == 4 and Or.ready() and tmpb.ready() and (a or Yf.ready()))
        k, bank, bf = Or.take()
        n = 0
        for j in range(4):
            w = Vt[:, j, P % 4, a * 128:a * 128 + 128]
            for part in range(2):
                n += 1
                sl = slice(OFF[j], OFF[j] + 512 - 128 * j)
                ev = put("tensor", lambda e, j=j, w=w, part=part, sl=sl, n=n: e.matmul(
                    bank[:, 128 * j:512], w, PTt[:, part, sl], start=n == 1, stop=n == 8),
                    list(bf) + [evv, d["pt_ev"][j]], chan("s_av") if n == 8 else None)
        PTb.free[tk] = [ev]
        if g % 8 == 7:
            Vb.free[vb] = [ev]
        main, other = (slice(0, 64), slice(64, 128)) if a == 0 else (slice(64, 128), slice(0, 64))
        xk, tm, xf = tmpb.take()
        e1 = put("scalar", lambda e: e.activation(tm[main, :], bank[other, :], ACT.Copy), [ev] + list(xf),
                 chan("s_ytmp"))
        if a == 0:
            d["Yf"] = Yf.take()
        else:
            d["Yf"] = hd[g - 1]["Yf"]
        yk, Yt, yfree = d["Yf"]

        def rest():
            e2 = put("vector", lambda e: e.tensor_tensor(Yt[main, :], bank[main, :], tm[main, :], ALU.add),
                     [e1] + list(yfree), chan("s_y"))
            Or.free[k] = [e2]
            tmpb.free[xk] = [e2]
            if a == 1:
                defer(1, lambda: split_y(e2))

        def split_y(e2):
            ok, Yo, of = Yb.take()
            e3 = copy("gpsimd", Yo[:, 0, :], Yt[:, :], [e2] + list(of), chan("s_yhi"))
            e4 = minus("gpsimd", Yo[:, 1, :], Yt[:, :], Yo[:, 0, :], [e3], chan("s_ylo"))
            Yf.free[yk] = [e4]
            Yslot[P] = (ok, Yo, e4)
        defer(1, rest)

    NG = B * H
    bg += ln1(0)
    bg += [vproj(0, t) for t in range(4)]
    bg += [proj(0, "k"), proj(0, "q")]
    need(("q", 0))
    for g in range(NG + LAG):
        P, a = g // 2, g % 2
        cur, prev = g < NG, 1 <= g <= NG
        if cur and a == 0:
            b = P // 8
            if P + 1 < NG // 2:
                bg += [proj(P + 1, "k"), proj(P + 1, "q")]
            if P % 8 == 2 and b + 1 < B:
                bg += ln1(b + 1)
            Hf = P // 4 + 1
            if Hf < 2 * B:
                bg.append(vproj(Hf, P % 4))
        for item in ORDER:
            if item == "bg":
                run_bg(1 + (len(bg) > 4))
                continue
            if item[0] == "S" and cur:
                scores(g, int(item[1]))
            elif item[0] == "T" and prev:
                transposes(g - 1, int(item[1]))
            elif item == "AV" and g >= LAG:
                av(g - LAG)
                if (g - LAG) % 4 == 3:
                    bg += [oproj((g - LAG) // 4, 0), oproj((g - LAG) // 4, 1)]
            tick()
    run_bg(len(bg))
    until(lambda: not due)
    cx.close()

    phase = [(chan(n), chan(n).n) for n in sems if sems[n].n]

    cx = ExitStack()
    w1 = sbf(root, "w1", [128, 2, 2, 1024], f32r)
    w2 = sbf(root, "w2", [128, 2, 2, 1024], f32r)
    s1c = sbf(root, "s1c", [128, 4, 8])
    hw = sbf(root, "hw", [128, 2, 8, 1024], f32r)
    rmax = [sbf(root, f"rmax{i}", [128, 16]) for i in range(2)]
    flag = [sbf(root, f"flag{i}", [128, 2]) for i in range(2)]
    XW = [sbf(cx, f"XW{i}", [128, 2, 2, 256], f32r) for i in range(3)]
    ctr = sbf(cx, "ctr", [128, 2, 2, 512], f32r)
    kT = sbf(cx, "kT", [128, 2, 2, 512], f32r)
    vT = sbf(cx, "vT", [128, 4, 2, 256], f32r)
    bqk = sbf(cx, "bqk", [128, 2, 2])
    bvb = sbf(cx, "bvb", [128, 256])
    mi = sbf(cx, "mi", [128, 256], i32)
    m01 = sbf(cx, "m01", [128, 256])
    mneg = sbf(cx, "mneg", [128, 256])
    xs = Ring([sbf(cx, f"xs{i}", [128, NT, 256]) for i in range(2)])
    xr = Ring([sbf(cx, f"xr{i}", [128, NT, 256]) for i in range(2)])
    xns = Ring([sbf(cx, f"xns{i}", [128, NT, 256]) for i in range(2)])
    XTs = Ring([sbf(cx, "XTs0", [128, 2, 2, 512], f32r)])
    qf = Ring([sbf(cx, "qf0", [128, 2, 512])])
    qT = Ring([sbf(cx, "qT0", [128, 2, 2, 512], f32r)])
    sf = Ring([sbf(cx, f"sf{i}", [128, 4, 64]) for i in range(2)])
    pf2 = [sbf(cx, f"pf{i}", [128, 4, 128]) for i in range(2)]
    pT = Ring([sbf(cx, f"pT{i}", [128, 2, 512], f32r) for i in range(2)])
    sm2 = Ring([sbf(cx, f"sm{i}", [128, NT, 9]) for i in range(2)])
    st2 = Ring([sbf(cx, f"st{i}", [128, 12]) for i in range(2)])
    stage = Ring([sbf(cx, f"stg{i}", [128, 1024]) for i in range(2)])

    for e in Q.q:
        Q.wait(e, phase)

    G8 = Ring(psum)

    e_xw = []
    for i, n in enumerate(("xwk", "xwv", "xwq")):
        e_xw.append(split_weight(stage, flat(XW[i], 0), flat(XW[i], 1), A[n], 512))
    e_small = [dma(bqk[:, :, :], A["bqk"], "s_bqk"), dma(bvb[:, :], A["bv"].broadcast_to([128, 256]), "s_bvb"),
               dma(mi[:, :], A["mask"], "s_mask"), dma(s1c[:, :, :], A["sc"], "s_sc")]
    def scratch(n):
        k, t, free = stage.take()
        return k, t[:, :].rearrange("p (a n) -> p a n", a=n), free

    ck, ctf, cf = scratch(2)
    ect = dma(ctf, A["ctxT"], "s_ctx", cf)
    e1 = copy("scalar", ctr[:, 0, :, :], ctf, [ect], chan("s_cthi"))
    e_ct = minus("vector", ctr[:, 1, :, :], ctf, ctr[:, 0, :, :], [e1], chan("s_ctlo"))
    stage.free[ck] = [e_ct]
    e1 = put("vector", lambda e: e.tensor_scalar(m01[:, :], mi[:, :], 0.0, None, ALU.not_equal), [e_small[2]],
             chan("s_m"))
    e_m = put("vector", lambda e: e.tensor_scalar(mneg[:, :], m01[:, :], 1.0, 1e9, ALU.subtract, ALU.mult), [e1],
              chan("s_m"))
    ek = []
    ck, kf, cf = scratch(2)
    for m in range(2):
        k, bank, bf = G8.take()
        for c in range(2):
            ev = mm3(bank[:, :], XW[0][:, 0, c, m * 128:m * 128 + 128], XW[0][:, 1, c, m * 128:m * 128 + 128],
                     ctr[:, 0, c, :], ctr[:, 1, c, :], c == 0, c == 1, e_xw[0] + [e_ct],
                     chan("s_xk") if c else None)
        e1 = put("vector", lambda e, m=m, bank=bank: e.tensor_scalar(kf[:, m, :], bank[:, :], bqk[:, 1, m:m + 1], None,
                 ALU.add), [ev, e_small[0]] + list(cf), chan("s_xkf"))
        G8.free[k] = [e1]
        e2 = copy("scalar", kT[:, 0, m, :], kf[:, m, :], [e1], chan("s_xkhi"))
        e3 = minus("vector", kT[:, 1, m, :], kf[:, m, :], kT[:, 0, m, :], [e2], chan("s_xklo"))
        ek.append(e3)
    stage.free[ck] = [e3]
    ev_ = []
    ck, vf_, cf = scratch(4)
    for w in range(4):
        k, bank, bf = G8.take()
        ws = slice(w * 128, w * 128 + 128)
        for c in range(2):
            ev = mm3(bank[:, 0:256], ctr[:, 0, c, ws], ctr[:, 1, c, ws], XW[1][:, 0, c, :], XW[1][:, 1, c, :],
                     c == 0, c == 1, e_xw[1] + [e_ct], chan("s_xv") if c else None)
        e1 = put("vector", lambda e, w=w, bank=bank: e.tensor_tensor(vf_[:, w, :], bank[:, 0:256], bvb[:, :], ALU.add),
                 [ev, e_small[1]] + list(cf), chan("s_xvf"))
        G8.free[k] = [e1]
        e2 = copy("scalar", vT[:, w, 0, :], vf_[:, w, :], [e1], chan("s_xvhi"))
        ev_.append(minus("vector", vT[:, w, 1, :], vf_[:, w, :], vT[:, w, 0, :], [e2], chan("s_xvlo")))
    stage.free[ck] = [ev_[-1]]
    for i in range(2):
        e_pz = put("gpsimd", lambda e, i=i: e.memset(pf2[i][:, :, :], 0.0), (), s_c)
    pf_free = [[e_pz], [e_pz]]
    X = [{} for _ in range(B)]
    e_x2 = {}

    def xa_load(b):
        d = X[b]
        d["x"] = xs.take()
        d["e_x"] = dma(d["x"][1][:, :, :], x1_v[b], f"s_xs{d['x'][0]}", d["x"][2])

    def xa_ln(b):
        d = X[b]
        d["xn"] = xns.take()
        d["sm"] = sm2.take()
        d["e_xn"] = layernorm("l2", d["x"][1], d["xn"][1], d["sm"][1], [d["e_x"]], d["xn"][2] + d["sm"][2])
        sm2.free[d["sm"][0]] = [d["e_xn"]]
        xs.free[d["x"][0]] = [d["e_xn"]]

    def xa_t(b):
        d = X[b]
        d["XT"] = XTs.take()
        d["e_XT"] = [transpose_split(d["xn"][1], d["e_xn"], d["XT"][1], d["XT"][2], G8, j) for j in range(2)]
        xns.free[d["xn"][0]] = d["e_XT"]

    def xa_q(b):
        d = X[b]
        d["qf"] = qf.take()
        d["qT"] = qT.take()
        Xt = d["XT"][1]
        d["e_q"] = []
        for m in range(2):
            k, bank, bf = G8.take()
            ms = slice(m * 128, m * 128 + 128)
            for c in range(2):
                ev = mm3(bank[:, :], XW[2][:, 0, c, ms], XW[2][:, 1, c, ms], Xt[:, 0, c, :], Xt[:, 1, c, :],
                         c == 0, c == 1, list(bf) + d["e_XT"] + e_xw[2], chan("s_xq") if c else None)
            qt, qtt = d["qf"][1], d["qT"][1]
            e1 = put("vector", lambda e, m=m, bank=bank, qt=qt: e.tensor_scalar(
                qt[:, m, :], bank[:, :], bqk[:, 0, m:m + 1], None, ALU.add), [ev] + d["qf"][2], chan("s_xqf"))
            G8.free[k] = [e1]
            e2 = copy("scalar", qtt[:, 0, m, :], qt[:, m, :], [e1] + d["qT"][2], chan("s_xqhi"))
            e3 = minus("gpsimd", qtt[:, 1, m, :], qt[:, m, :], qtt[:, 0, m, :], [e2] + d["qT"][2], chan("s_xqlo"))
            d["e_q"].append(e3)
        qf.free[d["qf"][0]] = [e3]
        XTs.free[d["XT"][0]] = [ev]

    def xa_s(b):
        d = X[b]
        k, bank, bf = G8.take()
        qtt = d["qT"][1]
        ks = slice(b * 64, b * 64 + 64)
        for t in range(4):
            ts = slice(t * 128, t * 128 + 128)
            for c in range(2):
                ev = mm3(bank[:, t * 64:t * 64 + 64], qtt[:, 0, c, ts], qtt[:, 1, c, ts], kT[:, 0, c, ks],
                         kT[:, 1, c, ks], c == 0, c == 1, list(bf) + d["e_q"] + ek,
                         chan("s_xS") if (t == 3 and c == 1) else None)
        qT.free[d["qT"][0]] = [ev]
        d["sf"] = sf.take()
        sk, st_, sfree = d["sf"]
        s4 = st_[:, :, :].rearrange("p t k -> p (t k)")
        e1 = put("vector", lambda e: e.tensor_tensor(s4, bank[:, 0:256], m01[:, :], ALU.mult), [ev, e_m] + list(sfree),
                 chan("s_xmask"))
        G8.free[k] = [e1]
        e1 = put("vector", lambda e: e.tensor_tensor(s4, s4, mneg[:, :], ALU.add), [e1], chan("s_xmask"))
        d["st"] = st2.take()
        stt = d["st"][1]
        e1 = put("vector", lambda e: e.tensor_reduce(stt[:, 0:4], st_[:, :, :], AX.X, ALU.max, negate=True),
                 [e1] + list(d["st"][2]), chan("s_xmask"))
        d["e_s"] = e1

    def xa_e(b):
        d = X[b]
        sk, st_, _ = d["sf"]
        tk, stt, _ = d["st"]
        pt = pf2[b % 2]
        o = 64 * (b % 2)
        for t in range(4):
            e2 = put("scalar", lambda e, t=t: e.activation(pt[:, t, o:o + 64], st_[:, t, :], ACT.Exp,
                     bias=stt[:, t:t + 1], scale=1.0, accum_out=stt[:, 4 + t:5 + t]), [d["e_s"]] + pf_free[b % 2],
                     chan("s_xe"))
        sf.free[sk] = [e2]
        e3 = put("vector", lambda e: e.reciprocal(stt[:, 8:12], stt[:, 4:8]), [e2], chan("s_xr"))
        for t in range(4):
            e4 = put("gpsimd", lambda e, t=t: e.tensor_scalar(pt[:, t, o:o + 64], pt[:, t, o:o + 64],
                     stt[:, 8 + t:9 + t], 1.0, ALU.mult, ALU.mult), [e3], chan("s_xn"))
        st2.free[tk] = [e4]
        d["e_p"] = e4

    def xa_pt(b):
        d = X[b]
        d["xr"] = xr.take()
        d["e_xr"] = dma(d["xr"][1][:, :, :], x1_v[b], f"s_xr{d['xr'][0]}", d["xr"][2])
        pt = pf2[b % 2]
        k, bank, bf = G8.take()
        for t in range(4):
            ev = put("tensor", lambda e, t=t: e.transpose(bank[:, t * 128:t * 128 + 128], pt[:, t, :],
                     ident[:, :]), list(bf) + [d["e_p"]], chan("s_xpT") if t == 3 else None)
        pf_free[b % 2] = [ev]
        d["pT"] = pT.take()
        pk, ptt, pfr = d["pT"]
        e1 = copy("scalar", ptt[:, 0, :], bank[:, :], [ev] + list(pfr), chan("s_xphi"))
        e2 = minus("vector", ptt[:, 1, :], bank[:, :], ptt[:, 0, :], [e1], chan("s_xplo"))
        G8.free[k] = [e2]
        d["e_pT"] = e2

    def xa_o(b):
        d = X[b]
        pk, ptt, _ = d["pT"]
        w = b // 2
        xk, xt, _ = d["xr"]
        es = []
        for tt in range(2):
            k, bank, bf = G8.take()
            for t in range(2):
                ts = slice((2 * tt + t) * 128, (2 * tt + t) * 128 + 128)
                ev = mm3(bank[:, t * 256:t * 256 + 256], ptt[:, 0, ts], ptt[:, 1, ts], vT[:, w, 0, :], vT[:, w, 1, :],
                         True, True, list(bf) + [d["e_pT"], ev_[w]], chan("s_xo") if t else None)
            xv = xt[:, 2 * tt:2 * tt + 2, :].rearrange("p t c -> p (t c)")
            e3 = put("vector", lambda e, bank=bank, xv=xv: e.tensor_tensor(xv, xv, bank[:, :], ALU.add),
                     [ev, d["e_xr"]], chan("s_xacc2"))
            G8.free[k] = [e3]
            es.append(e3)
        pT.free[pk] = [ev]
        e_x2[b] = dma(x2_v[b], xt[:, :, :], f"s_x2st{xk}", es)
        xr.free[xk] = [e_x2[b]]

    rm = [rmax[0], 0, None]
    hwf = lambda i, m: hw[:, i, m, :]
    e_h1 = []
    weights = [lambda: e_w1.extend(split_weight(stage, flat(w1, 0), flat(w1, 1), A["w1"], 2048, rest_max=rm)),
               lambda: e_w2.extend(split_weight(stage, flat(w2, 0), flat(w2, 1), A["w2"], 2048, rest_max=rm))]
    weights += [lambda m=m: e_h1.append(split_weight(stage, hwf(0, m), hwf(1, m), A["h1"][m], 1024, rest_max=rm))
                for m in range(8)]
    e_w1, e_w2 = [], []
    STAGES = [xa_load, xa_ln, xa_t, xa_q, xa_s, xa_e, xa_pt, xa_o]
    for s in range(B + len(STAGES) - 1):
        for k in reversed(range(len(STAGES))):
            if 0 <= s - k < B:
                STAGES[k](s - k)
        if s >= 1 and weights:
            weights.pop(0)()
    for w in weights:
        w()
    e_f1 = rest_flag(rm, flag[0], "s_flag")
    cx.close()
    phase = [(chan(n), chan(n).n) for n in sems if sems[n].n]

    cx = ExitStack()
    w3 = sbf(root, "w3", [128, 2, 8, 256], f32r)
    Hb = sbf(root, "Hb", [128, 2, 8, 512], f32r)
    stage = Ring([sbf(root, f"stgf{i}", [128, 1024]) for i in range(2)])
    s3b = sbf(root, "s3b", [128, 256])
    xs = Ring([sbf(cx, f"xf{i}", [128, NT, 256]) for i in range(2)])
    xns = Ring([sbf(cx, f"xnf{i}", [128, NT, 256]) for i in range(1)])
    XTs = Ring([sbf(cx, f"XTf{i}", [128, 2, 2, 512], f32r) for i in range(2)])
    sm2 = Ring([sbf(cx, f"smf{i}", [128, NT, 9]) for i in range(1)])
    gt = Ring([sbf(cx, f"gt{i}", [128, 512]) for i in range(2)])
    ht = Ring([sbf(cx, f"ht{i}", [128, 512]) for i in range(2)])
    hl_tiles = [sbf(cx, f"hl{i}", [128, 512]) for i in range(3)]
    ot = Ring([sbf(cx, f"ot{i}", [128, 512]) for i in range(2)])
    go_ = Ring([sbf(cx, f"go{i}", [128, 512]) for i in range(2)])

    for e in Q.q:
        Q.wait(e, phase)
    e_s3 = dma(s3b[:, :], A["s3"].broadcast_to([128, 256]), "s_s3")
    G8 = Ring(psum)
    regs = [None]

    def load_flag(i, ev):
        def go(e):
            if regs[0] is None:
                regs[0] = e.alloc_register("low_parts")
            e.reg_load(regs[0], flag[i][0:1, 1:2].bitcast(i32))
        put("tensor", go, [ev])

    def product(parts, waits, last_sig, lo_first):
        n = len(parts)

        def mm(e, dst, w, x, start, stop):
            a, b = (w, x) if lo_first else (x, w)
            return e.matmul(dst, a, b, start=start, stop=stop)
        for i, (dst, wh, wl, xh, xl, ws) in enumerate(parts):
            put("tensor", lambda e, dst=dst, wh=wh, xh=xh, i=i: mm(e, dst, wh, xh, i == 0, False),
                list(waits) + list(ws))
            if i < n - 1:
                put("tensor", lambda e, dst=dst, wh=wh, xl=xl: mm(e, dst, wh, xl, False, False))

        def low(e):
            with e.If_ne(regs[0], 0):
                for dst, wh, wl, xh, xl, _ in parts:
                    mm(e, dst, wl, xh, False, False)
        put("tensor", low)
        dst, wh, wl, xh, xl, _ = parts[-1]
        return put("tensor", lambda e: mm(e, dst, wh, xl, False, True), (), last_sig)

    load_flag(0, e_f1)
    rm = [rmax[1], 0, None]
    e_w3 = split_weight(stage, flat(w3, 0), flat(w3, 1), A["w3"], 2048, rest_max=rm)
    F = {}

    def f_load(b):
        d = F[b] = {}
        d["x"] = xs.take()
        d["e_x"] = dma(d["x"][1][:, :, :], x2_v[b], f"s_xf{d['x'][0]}", d["x"][2] + [e_x2[b]])

    def f_ln(b):
        d = F[b]
        d["xn"] = xns.take()
        d["sm"] = sm2.take()
        d["e_xn"] = layernorm("l3", d["x"][1], d["xn"][1], d["sm"][1], [d["e_x"]], d["xn"][2] + d["sm"][2])
        sm2.free[d["sm"][0]] = [d["e_xn"]]
        xs.free[d["x"][0]] = [d["e_xn"]]

    def f_xt(b):
        d = F[b]
        d["XT"] = XTs.take()
        d["e_XT"] = [transpose_split(d["xn"][1], d["e_xn"], d["XT"][1], d["XT"][2], G8, j) for j in range(2)]
        xns.free[d["xn"][0]] = d["e_XT"]

    e_H = [None] * 8
    H_free = [[] for _ in range(8)]

    def f_w(b, m):
        d = F[b]
        Xt = d["XT"][1]
        ms = slice(m * 128, m * 128 + 128)
        res = []
        for W, ew in ((w1, e_w1), (w2, e_w2)):
            k, bank, bf = G8.take()
            ev = product([(bank[:, :], W[:, 0, c, ms], W[:, 1, c, ms], Xt[:, 0, c, :], Xt[:, 1, c, :], ())
                          for c in range(2)], list(bf) + d["e_XT"] + ew, chan("s_gu"), True)
            res.append((k, bank, ev))
        (k1, bk1, ev1), (k2, bk2, ev2) = res
        if m == 7:
            XTs.free[d["XT"][0]] = [ev2]
        gk, g_, gf = gt.take()
        e1 = put("scalar", lambda e: e.activation(g_[:, :], bk1[:, :], ACT.Silu, scale=s1c[:, 0, m:m + 1]),
                 [ev1] + list(gf), chan("s_silu"))
        G8.free[k1] = [e1]
        hk, h_, hf = ht.take()
        e2 = put("vector", lambda e: e.scalar_tensor_tensor(h_[:, :], bk2[:, :], s1c[:, 1, m:m + 1], g_[:, :],
                 ALU.mult, ALU.mult), [ev2, e1] + list(hf), chan("s_h"))
        G8.free[k2] = [e2]
        gt.free[gk] = [e2]
        e3 = copy("scalar", Hb[:, 0, m, :], h_[:, :], [e2] + H_free[m], chan("s_hhi"))
        e4 = minus("vector", Hb[:, 1, m, :], h_[:, :], Hb[:, 0, m, :], [e3] + H_free[m], chan("s_hlo"))
        ht.free[hk] = [e4]
        e_H[m] = e4

    def hidden(m, e_h, src, e_in):
        k, bank, bf = G8.take()
        sl = [slice(c * 128, c * 128 + 128) for c in range(8)]
        ev = product([(bank[:, :], hw[:, 0, m, sl[c]], hw[:, 1, m, sl[c]], src[0][:, c, :], src[1][:, c, :],
                       [e_in[c]]) for c in range(8)], list(bf) + e_h[m], chan("s_hid"), True)
        return k, bank, ev

    e_hst = {}

    def f_h(b, m):
        k, bank, ev = hidden(m, e_h1, (Hb[:, 0], Hb[:, 1]), e_H)
        if m == 7:
            for c in range(8):
                H_free[c] = [ev]
        ok, o_, of = go_.take()
        e1 = put("scalar", lambda e: e.activation(o_[:, :], bank[:, :], ACT.Gelu, scale=s1c[:, 2, m:m + 1]),
                 [ev] + list(of), chan("s_gelu"))
        G8.free[k] = [e1]
        e_hst[b, m] = dma(h_d[b, m], o_[:, :], f"s_hst{ok}", [e1])
        go_.free[ok] = [e_hst[b, m]]
        return ev

    f_load(0)
    f_ln(0)
    f_xt(0)
    f_load(1)
    e_hw_last = [None] * 8
    for b in range(B):
        for m in range(8):
            f_w(b, m)
        e_gu_last = (chan("s_gu"), chan("s_gu").n)
        if b + 1 < B:
            f_ln(b + 1)
            if b + 2 < B:
                f_load(b + 2)
        for m in range(8):
            e_hw_last[m] = f_h(b, m)
            if m == 4 and b + 1 < B:
                f_xt(b + 1)

    Gb = [w[:, :, :, :].rearrange("p a k f -> p (a k f)").rearrange("p (c n) -> p c n", c=8) for w in (w1, w2)]
    e_G = [None] * 8
    G_free = [[e_gu_last] for _ in range(8)]
    hl = Ring([t[:, :] for t in hl_tiles])

    def g_load(b, m):
        k, t, f = hl.take()
        e0 = dma(t, h_d[b, m], f"s_hl{k}", list(f) + [e_hst[b, m]])
        e1 = copy("gpsimd", Gb[0][:, m, :], t, [e0] + G_free[m], chan("s_h2hi"))
        e2 = minus("vector", Gb[1][:, m, :], t, Gb[0][:, m, :], [e1] + G_free[m], chan("s_h2lo"))
        hl.free[k] = [e2]
        e_G[m] = e2

    for m in range(8):
        g_load(0, m)
    e_h2 = [split_weight(stage, hwf(0, m), hwf(1, m), A["h2"][m], 1024, waits=[e_hw_last[m]],
            eng=("scalar", "vector"), rest_max=rm) for m in range(8)]
    load_flag(1, rest_flag(rm, flag[1], "s_flag"))

    def g_h(m):
        k, bank, ev = hidden(m, e_h2, Gb, e_G)
        if m == 7:
            for c in range(8):
                G_free[c] = [ev]
        gk, g_, gf = gt.take()
        e1 = put("scalar", lambda e: e.activation(g_[:, :], bank[:, :], ACT.Gelu, scale=s1c[:, 3, m:m + 1]),
                 [ev] + list(gf), chan("s_gelu2"))
        G8.free[k] = [e1]
        e2 = copy("gpsimd", Hb[:, 0, m, :], g_[:, :], [e1] + H_free[m], chan("s_ghi"))
        e3 = minus("vector", Hb[:, 1, m, :], g_[:, :], Hb[:, 0, m, :], [e2] + H_free[m], chan("s_glo"))
        gt.free[gk] = [e3]
        e_H[m] = e3

    xg = {}

    def g_out(b, tt):
        k, bank, bf = G8.take()
        for t in range(2):
            ts = slice((2 * tt + t) * 128, (2 * tt + t) * 128 + 128)
            ev = product([(bank[:, t * 256:t * 256 + 256], w3[:, 0, c, :], w3[:, 1, c, :], Hb[:, 0, c, ts],
                           Hb[:, 1, c, ts], [e_H[c]]) for c in range(8)], list(bf) + e_w3, chan("s_out"), False)
        if tt == 1:
            for c in range(8):
                H_free[c] = [ev]
        ok, o_, of = ot.take()
        es = []
        for t in range(2):
            e1 = put("vector", lambda e, t=t: e.tensor_tensor(o_[:, t * 256:t * 256 + 256],
                     bank[:, t * 256:t * 256 + 256], s3b[:, :], ALU.mult), [ev, e_s3] + list(of), chan("s_fs"))
        G8.free[k] = [e1]
        xk, xt, _, ex = xg[b]
        xv = xt[:, 2 * tt:2 * tt + 2, :].rearrange("p t c -> p (t c)")
        e2 = put("vector", lambda e: e.tensor_tensor(o_[:, :], o_[:, :], xv, ALU.add), [e1, ex], chan("s_fs"))
        e3 = dma(out_v[b][:, 2 * tt:2 * tt + 2, :].rearrange("p t c -> p t c"),
                 o_[:, :].rearrange("p (t c) -> p t c", t=2), f"s_final{ok}", [e2])
        ot.free[ok] = [e3]
        if tt == 1:
            xs.free[xk] = [e2]

    for b in range(B):
        k, t, f = xs.take()
        xg[b] = (k, t, f, dma(t[:, :, :], x2_v[b], f"s_xf{k}", list(f) + [e_x2[b]]))
        for m in range(8):
            g_h(m)
        if b + 1 < B:
            for m in range(8):
                g_load(b + 1, m)
        g_out(b, 0)
        g_out(b, 1)
    cx.close()
    Q.wait("sync", [(c, c.n) for n, c in sems.items() if n[:-1] in ("s_final", "s_x1st", "s_x2st", "s_hst")])

    with nc.Block() as block:
        @block.sync
        def _(e):
            for f in Q.q["sync"]:
                f(e)

        @block.gpsimd
        def _(e):
            for f in Q.q["gpsimd"]:
                f(e)

        @block.scalar
        def _(e):
            for f in Q.q["scalar"]:
                f(e)

        @block.vector
        def _(e):
            for f in Q.q["vector"]:
                f(e)

        @block.tensor
        def _(e):
            for f in Q.q["tensor"]:
                f(e)
    root.close()


def kernel(**inputs):
    import numpy as np
    import concourse.bacc as _bacc
    from concourse import mybir as _mybir
    from concourse.bass_utils import run_bass_kernel_spmd as _run

    I = {k: np.asarray(v) for k, v in inputs.items()}

    def kt(w):
        o, i = w.shape
        return w.T.reshape(i // 128, 128, o).transpose(1, 0, 2).reshape(128, -1)

    def mkt(w):
        o, i = w.shape
        return w.T.reshape(i // 128, 128, o // 128, 128).transpose(2, 1, 0, 3).reshape(o // 128, 128, i)

    col = lambda v: v.reshape(-1, 128).T
    a = {
        "x": I["x"],
        "wq": kt(I["L0_attn_w_q"].reshape(1024, 256)),
        "wk": kt(I["L0_attn_w_k"].reshape(1024, 256)),
        "wv": kt(I["L0_attn_w_v"].reshape(1024, 256)),
        "wo": kt(I["L0_attn_w_o"].T),
        "xwq": kt(I["L0_xattn_Wq"]),
        "xwk": kt(I["L0_xattn_Wk"]),
        "xwv": kt(I["L0_xattn_Wv"]),
        "bqk": np.stack([col(I["L0_xattn_bq"]), col(I["L0_xattn_bk"])], 1),
        "bv": I["L0_xattn_bv"].reshape(1, 256),
        "ctxT": I["ctx_1024"].reshape(512, 256).T.reshape(2, 128, 512).transpose(1, 0, 2),
        "mask": I["mask_SxS2_ik1"].reshape(4, 128, 64).transpose(1, 0, 2).reshape(128, 256),
        "w1": kt(I["L0_ffn_w1_w"]),
        "w2": kt(I["L0_ffn_w2_w"]),
        "h1": mkt(I["L0_ffn_h1_w"]),
        "h2": mkt(I["L0_ffn_h2_w"]),
        "w3": kt(I["L0_ffn_w3_w"]),
        "sc": np.stack([col(I[f"L0_ffn_{n}_s"]) for n in ("w1", "w2", "h1", "h2")], 1),
        "s3": I["L0_ffn_w3_s"].reshape(1, 256),
    }
    a = {k: np.ascontiguousarray(v) for k, v in a.items()}
    nc = _bacc.Bacc("TRN2", target_bir_lowering=False, num_devices=1)
    aps = {k: nc.dram_tensor(f"in_{k}", v.shape, _mybir.dt.from_np(v.dtype), kind="ExternalInput").ap()
           for k, v in a.items()}
    out = nc.dram_tensor("out_0", (B, T, C), _mybir.dt.float32, kind="ExternalOutput").ap()
    program(nc, aps, out)
    r = _run(nc, [{f"in_{k}": v for k, v in a.items()}], core_ids=[0])
    return r.results[0]["out_0"]
```

```python
import concourse.bass as bass
from concourse import mybir
from contextlib import ExitStack


class Chan:

    def __init__(self, sem, step=1):
        self.sem, self.step, self.n = sem, step, 0


class Queues:

    def __init__(self):
        self.q = {k: [] for k in ("tensor", "vector", "scalar", "gpsimd", "sync")}
        self.seen = {k: {} for k in self.q}

    def wait(self, eng, events):
        for ev in events:
            if ev is None:
                continue
            ch, n = ev
            if self.seen[eng].get(ch, 0) < n:
                self.seen[eng][ch] = n
                self.q[eng].append(lambda e, ch=ch, n=n: e.wait_ge(ch.sem, n))

    def put(self, eng, fn, waits=(), sig=None):
        self.wait(eng, waits)
        if sig is None:
            self.q[eng].append(fn)
            return None
        sig.n += sig.step
        self.q[eng].append(lambda e: fn(e).then_inc(sig.sem, sig.step))
        return (sig, sig.n)


class Ring:

    def __init__(self, tiles, free=None):
        self.tiles, self.free, self.i = tiles, free or [[] for _ in tiles], -1

    def ready(self):
        return self.free[(self.i + 1) % len(self.tiles)] is not None

    def take(self):
        self.i += 1
        k = self.i % len(self.tiles)
        f, self.free[k] = self.free[k], None
        assert f is not None
        return k, self.tiles[k], f


B, T, C, H = 8, 512, 256, 16
NT = 4
S2 = 64
NEG = -1e30
DX, DN, DL, LAG = 3, 1, 1, 2
ORDER = ("T0", "S3", "AV", "S2", "S1", "T1", "bg", "S0", "T2", "bg")
EPS = 1e-5


def program(nc, A, out):
    RMAX = bass.bass_isa.ReduceOp.max
    f32, f32r, i32 = mybir.dt.float32, mybir.dt.float32r, mybir.dt.int32
    ACT, ALU, AX = mybir.ActivationFunctionType, mybir.AluOpType, mybir.AxisListType
    Q = Queues()
    put = Q.put
    root = ExitStack()
    x1_d = nc.dram_tensor("x1_scratch", (B, T, C), f32, kind="Internal").ap()
    x2_d = nc.dram_tensor("x2_scratch", (B, T, C), f32, kind="Internal").ap()
    h_d = nc.dram_tensor("h_scratch", (B, 8, 128, T), f32, kind="Internal").ap()
    sems = {}

    def chan(name, step=1):
        if name not in sems:
            sems[name] = Chan(root.enter_context(nc.semaphore(name)), step)
        return sems[name]

    def dma(dst, src, name, waits=()):
        return put("gpsimd" if "kswap" in name else "sync", lambda e: e.dma_start(dst, src), waits, chan(name, 16))

    psum = [root.enter_context(nc.psum_tensor(f"bank{i}", [128, 512], f32)) for i in range(8)]

    def sbf(cx, name, shape, dt=f32):
        return cx.enter_context(nc.sbuf_tensor(name, shape, dt))

    ident = sbf(root, "ident", [128, 128])
    identr = sbf(root, "identr", [128, 128], f32r)
    s_c = chan("s_const")
    e0 = put("gpsimd", lambda e: e.memset(ident[:, :], 0.0), (), s_c)
    e_id = put("gpsimd", lambda e: e.affine_select(out=ident[:, :], in_=ident[:, :], compare_op=ALU.not_equal,
               fill=1.0, base=0, pattern=[[-1, 128]], channel_multiplier=1), [e0], s_c)
    e_idr = put("scalar", lambda e: e.activation(identr[:, :], ident[:, :], ACT.Copy), [e_id], chan("s_identr"))

    def copy(eng, dst, src, waits, sig, scale=1.0):
        if eng == "scalar":
            return put(eng, lambda e: e.activation(dst, src, ACT.Copy, scale=scale), waits, sig)
        return put(eng, lambda e: e.tensor_scalar(dst, src, scale, 1.0, ALU.mult, ALU.mult), waits, sig)

    def minus(eng, dst, a, b, waits, sig):
        return put(eng, lambda e: e.tensor_tensor(dst, a, b.bitcast(f32), ALU.subtract), waits, sig)

    def split_weight(ring, dst_hi, dst_lo, src, n, scale=1.0, after=(), eng=("scalar", "vector"), rest=None):
        evs = []
        width = ring.tiles[0].shape[-1]
        for a in range(0, n, width):
            m = min(width, n - a)
            k, st, free = ring.take()
            e_ld = dma(st[:, 0:m], src[:, a:a + m], f"s_wld{k}", list(free))
            e_hi = copy(eng[0], dst_hi[:, a:a + m], st[:, 0:m], [e_ld] + list(after), chan("s_whi_" + eng[0]), scale)
            e_lo = put(eng[1], lambda e, a=a, m=m, st=st: e.scalar_tensor_tensor(
                dst_lo[:, a:a + m], st[:, 0:m], scale, dst_hi[:, a:a + m].bitcast(f32), ALU.mult, ALU.subtract),
                [e_hi], chan("s_wlo_" + eng[1])) if scale != 1.0 else minus(eng[1], dst_lo[:, a:a + m], st[:, 0:m], dst_hi[:, a:a + m], [e_hi],
                         chan("s_wlo_" + eng[1]))
            ring.free[k] = [e_lo]
            evs += [e_lo]
            if rest is not None:
                largest(rest, dst_lo[:, a:a + m].bitcast(f32), [e_lo])
        return evs

    def largest(rest, src, waits):
        tile, c, _ = rest
        rest[1] = c + 1
        rest[2] = put("vector", lambda e: e.tensor_reduce(tile[:, c:c + 1], src, AX.X, ALU.max,
                      apply_absolute_value=True), waits, chan("s_rest"))
        return rest[2]

    def rest_flag(rest, flag, name):
        tile, n, ev = rest
        e1 = put("vector", lambda e: e.tensor_reduce(flag[:, 0:1], tile[:, 0:n], AX.X, ALU.max), [ev],
                 chan("s_rest"))
        return put("gpsimd", lambda e: e.partition_all_reduce(flag[:, 1:2], flag[:, 0:1], 128, RMAX), [e1],
                   chan(name))

    def mm3(dst, whi, wlo, xhi, xlo, first, last, waits, sig):
        put("tensor", lambda e: e.matmul(dst, whi, xhi, start=first, stop=False), waits)
        put("tensor", lambda e: e.matmul(dst, whi, xlo, start=False, stop=False))
        return put("tensor", lambda e: e.matmul(dst, wlo, xhi, start=False, stop=last), (), sig)

    at_once = lambda n, fn: fn()

    def layernorm(x, xn, small, waits, free, later=at_once):
        st = small[:, :, 0:6]
        mv = small[:, :, 6:8]
        rs = small[:, :, 8:9]
        s = chan("s_ln")
        final = []

        def sums(t):
            return put("vector", lambda e: e.bn_stats(st[:, t, :], x[:, t, :]), list(waits) + list(free), s)

        def scale(ev):
            for t in range(NT):
                ev = put("vector", lambda e, t=t: e.bn_aggr(mv[:, t, :], st[:, t, :]), [ev], s)
            ev = put("vector", lambda e: e.tensor_scalar(rs, mv[:, :, 1:2], EPS, None, ALU.add), [ev], s)
            ev = put("gpsimd", lambda e: e.tensor_tensor(rs, rs, half[:, :].rearrange("p (t o) -> p t o", o=1),
                     ALU.pow), [ev, e_half], chan("s_rstd"))
            later(4, lambda: norm(ev, 0))

        def norm(ev, t0):
            for t in range(t0, t0 + 2):
                ev2 = put("vector", lambda e, t=t: e.tensor_scalar(xn[:, t, :], x[:, t, :], mv[:, t, 0:1],
                          rs[:, t, :], ALU.subtract, ALU.mult), [ev], s)
            if t0:
                final.append(ev2)
            else:
                later(3, lambda: norm(ev, 2))

        def begin(t0):
            for t in range(t0, t0 + 2):
                ev = sums(t)
            later(3, (lambda: scale(ev)) if t0 else (lambda: begin(2)))
        begin(0)
        return final

    def transpose_split(xn, e_xn, XT, free, ring, j, later=None, then=None):
        k, bank, bf = ring.take()
        for t in range(NT):
            ev = put("tensor", lambda e, t=t: e.transpose(bank[:, t * 128:t * 128 + 128],
                     xn[:, t, j * 128:j * 128 + 128], ident[:, :]), [e_xn, e_id] + list(bf),
                     chan("s_xnT") if t == NT - 1 else None)
        e_hi = copy("scalar", XT[:, 0, j, :], bank[:, :], [ev] + list(free), chan("s_xhi"))
        def rest():
            e_lo = minus("vector", XT[:, 1, j, :], bank[:, :], XT[:, 0, j, :], [e_hi] + list(free), chan("s_xlo"))
            ring.free[k] = [e_lo]
            if then:
                then(e_lo)
            return e_lo
        return later(1, rest) if later else rest()

    half = sbf(root, "half", [128, NT])
    e_half = put("gpsimd", lambda e: e.memset(half[:, :], -0.5), (), s_c)

    cx = ExitStack()
    cmask = sbf(cx, "cmask", [128, 128])
    cmaskr = sbf(cx, "cmaskr", [128, 128], f32r)
    e0 = put("gpsimd", lambda e: e.memset(cmask[:, :], 0.0), (), s_c)
    e0 = put("gpsimd", lambda e: e.affine_select(out=cmask[:, :], in_=cmask[:, :], compare_op=ALU.is_ge, fill=NEG,
             base=0, pattern=[[-1, 128]], channel_multiplier=1), [e0], s_c)
    e_cm = put("scalar", lambda e: e.activation(cmaskr[:, :], cmask[:, :], ACT.Copy), [e0], chan("s_identr"))
    Wq = sbf(cx, "Wq", [128, 2, 2, 1024], f32r)
    Wk = sbf(cx, "Wk", [128, 2, 2, 1024], f32r)
    Wv = sbf(cx, "Wv", [128, 2, 2, 1024], f32r)
    Wo = sbf(cx, "Wo", [128, 2, 8, 256], f32r)
    XTb = [sbf(cx, f"XT{i}", [128, 2, 2, 512], f32r) for i in range(2)]
    Kb = Ring([sbf(cx, f"K{i}", [128, 2, 2, 512], f32r) for i in range(2)])
    Qb = Ring([sbf(cx, f"Q{i}", [128, 2, 512], f32r) for i in range(2)])
    Vb = Ring([sbf(cx, f"V{i}", [128, NT, 4, 256], f32r) for i in range(2)])
    Pb = Ring([sbf(cx, f"P{i}", [128, 1280]) for i in range(2)])
    PTb = Ring([sbf(cx, f"PT{i}", [128, 2, 1280], f32r) for i in range(2)])
    Yb = Ring([sbf(cx, f"Y{i}", [128, 2, 512], f32r) for i in range(4)])
    Yf = Ring([sbf(cx, "Yf0", [128, 512])])
    tmpb = Ring([sbf(cx, "ytmp", [128, 512])])
    xb = [sbf(cx, f"x{i}", [128, NT, 256]) for i in range(2)]
    xn = sbf(cx, "xn", [128, NT, 256])
    small = sbf(cx, "lnsmall", [128, NT, 9])
    stats = [sbf(cx, f"stats{i}", [128, 12]) for i in range(4)]
    stage = Ring([Pb.tiles[0][:, 0:1024], Pb.tiles[1][:, 0:1024], xb[1][:, :, :].rearrange("p t c -> p (t c)")])

    x_in = A["x"].rearrange("b (t p) c -> b p t c", p=128)
    x1_v = x1_d.rearrange("b (t p) c -> b p t c", p=128)
    x2_v = x2_d.rearrange("b (t p) c -> b p t c", p=128)
    out_v = out.rearrange("b (t p) c -> b p t c", p=128)

    Sr = Ring([psum[i] for i in (0, 1, 2)])
    Tr = Ring([psum[i] for i in (3, 4)])
    Or = Ring([psum[5]])
    Gr = Ring([psum[i] for i in (6, 7)])

    e_x = {0: dma(xb[0][:, :, :], x_in[0], "s_xld0")}
    flat = lambda w, i: w[:, i, :, :].rearrange("p k f -> p (k f)")

    slot, due, bg, done = [0], [], [], set()

    def defer(n, fn):
        due.append((slot[0] + n, fn))

    def tick():
        slot[0] += 1
        now = [d for d in due if d[0] <= slot[0]]
        due[:] = [d for d in due if d[0] > slot[0]]
        for _, fn in now:
            fn()

    def until(cond):
        while not cond():
            assert due
            tick()

    def run_bg(n):
        for _ in range(n):
            if bg:
                tag, fn = bg.pop(0)
                fn()
                done.add(tag)
                tick()

    def need(tag):
        while tag not in done:
            assert bg, tag
            run_bg(1)

    e_XT, XT_free, e_xacc = {}, [[], []], {}
    pairQ, pairK, halfV = {}, {}, {}

    def ln1(b):
        def load():
            if b not in e_x:
                e_x[b] = dma(xb[b % 2][:, :, :], x_in[b], f"s_xld{b % 2}",
                             e_x1free if b == 1 else [e_st1[b - 2]])
        def norm():
            load()
            if b:
                until(lambda: len(e_XT[b - 1]) == 2)
            lns[b] = layernorm(xb[b % 2], xn, small, [e_x[b]], [e_XT[b - 1][1]] if b else [],
                               later=defer if b else at_once)
        def tr(j):
            until(lambda: lns[b] and Gr.ready())
            e_xn[b] = lns[b][0]
            transpose_split(xn, e_xn[b], XTb[b % 2], XT_free[b % 2], Gr, j, later=defer,
                            then=e_XT.setdefault(b, []).append)
        return [(("ln", b), norm), (("xt0", b), lambda: tr(0)), (("xt", b), lambda: tr(1))]
    e_xn, e_st1, lns = {}, {}, {}

    def proj(P, which):
        b, p = P // 8, P % 8
        def go():
            X = XTb[b % 2]
            until(lambda: len(e_XT.get(b, ())) == 2 and Gr.ready())
            W, ew = (Wq, e_wq) if which == "q" else (Wk, e_wk)
            k, bank, bf = Gr.take()
            fs = slice(p * 128, p * 128 + 128)
            for c in range(2):
                ev = mm3(bank[:, :], W[:, 0, c, fs], W[:, 1, c, fs], X[:, 0, c, :], X[:, 1, c, :],
                         c == 0, c == 1, list(bf) + e_XT[b] + ew, chan("s_qk") if c == 1 else None)
            rk, Rt, rf = (Kb if which == "k" else Qb).take()
            T1 = Rt[:, 0] if which == "k" else Rt[:, :, :]
            own = (slice(0, 64), slice(64, 128))
            for a in range(2):
                e1 = copy("scalar", T1[own[a], a, :], bank[own[a], :], [ev] + list(rf), chan("s_qkhi"))

            def rest():
                for a in range(2):
                    e2 = minus("vector", T1[own[1 - a], a, :], bank[own[a], :], T1[own[a], a, :], [e1] + list(rf),
                               chan("s_qklo"))
                Gr.free[k] = [e2]
                if which == "q":
                    pairQ[P] = (rk, Rt, e2)
                    return
                for a in range(2):
                    e3 = dma(Rt[own[1 - a], 1], T1[own[a]], f"s_kswap{rk}", [e2] + list(rf))
                pairK[P] = (rk, Rt, e3)
            defer(1, rest)
            if P % 8 == 7 and which == "q":
                XT_free[b % 2] = [ev]
        return ((which, P), go)

    def vproj(Hf, t):
        b, hh = Hf // 2, Hf % 2
        def go():
            until(lambda: len(e_XT.get(b, ())) == 2 and Gr.ready() and Vb.ready() | (t > 0))
            if t == 0:
                halfV[Hf] = [*Vb.take(), None]
            kb, Vt, vf, _ = halfV[Hf]
            X = XTb[b % 2]
            k, bank, bf = Gr.take()
            ts = slice(t * 128, t * 128 + 128)
            fs = slice(hh * 512, hh * 512 + 512)
            for c in range(2):
                ev = mm3(bank[:, :], X[:, 0, c, ts], X[:, 1, c, ts], Wv[:, 0, c, fs], Wv[:, 1, c, fs],
                         c == 0, c == 1, list(bf) + e_XT[b] + e_wv, chan("s_v") if c == 1 else None)
            src = bank[:, :].rearrange("p (q a d) -> p q a d", q=4, a=2)
            v4 = Vt[:, t, :, :].rearrange("p q (s d) -> p q s d", d=64)
            e1 = copy("scalar", v4[:, :, 0:4:3, :], src, [ev] + list(vf), chan("s_vhi"))

            def rest():
                e2 = minus("vector", v4[:, :, 1:3, :], src, v4[:, :, 0:4:3, :], [e1] + list(vf), chan("s_vlo"))
                Gr.free[k] = [e2]
                halfV[Hf][3] = e2
            defer(1, rest)
        return (("v", Hf, t), go)

    Yslot = {}

    def oproj(Qr, tt):
        b = Qr // 4
        def go():
            until(lambda: 2 * Qr + 1 in Yslot and Gr.ready())
            k, bank, bf = Gr.take()
            for t in (2 * tt, 2 * tt + 1):
                o = bank[:, (t % 2) * 256:(t % 2) * 256 + 256]
                ts = slice(t * 128, t * 128 + 128)
                for i in range(2):
                    P = 2 * Qr + i
                    yk, Yt, ey = Yslot[P]
                    ev = mm3(o, Yt[:, 0, ts], Yt[:, 1, ts], Wo[:, 0, P % 8, :], Wo[:, 1, P % 8, :],
                             i == 0, i == 1, list(bf) + [ey] + e_wo, chan("s_o") if i == 1 else None)
            if tt == 1:
                for i in range(2):
                    Yb.free[Yslot[2 * Qr + i][0]] = [ev]
            xt = xb[b % 2][:, 2 * tt:2 * tt + 2, :].rearrange("p t c -> p (t c)")
            e2 = put("vector", lambda e: e.tensor_tensor(xt, xt, bank[:, :], ALU.add), [ev, e_xn[b]]
                     + ([e_xacc[b, tt]] if (b, tt) in e_xacc else []), chan("s_xacc"))
            Gr.free[k] = [e2]
            e_xacc[b, tt] = e2
            if Qr % 4 == 3 and tt == 1:
                e_st1[b] = dma(x1_v[b], xb[b % 2][:, :, :], f"s_x1st{b % 2}", [e2])
        return (("o", Qr, tt), go)

    OFF = {0: 0, 1: 512, 3: 896, 2: 1024}
    POFF = {3: 0, 2: 512, 1: 896, 0: 1152}
    hd = {}

    def scores(g, i):
        P, a = g // 2, g % 2
        if i == 3:
            need(("q", P)), need(("k", P))
            until(lambda: P in pairQ and P in pairK and Pb.ready())
            pk, Pt, pf = Pb.take()
            hd[g] = dict(P=(pk, Pt, pf), exp={})
        d = hd[g]
        qb, Qt, eq = pairQ[P]
        kb, Kt, ek = pairK[P]
        until(Sr.ready)
        k, bank, bf = Sr.take()
        n = 128 * (i + 1)
        qs = slice(i * 128, i * 128 + 128)
        for o in range(2):
            put("tensor", lambda e, o=o: e.matmul(bank[:, 0:n], Qt[:, a, qs], Kt[:, o, a, 0:n], start=o == 0,
                stop=False), list(bf) + [eq, ek])
        ev = put("tensor", lambda e: e.matmul(bank[:, n - 128:n], identr[:, :], cmaskr[:, :], start=False,
                 stop=True), [e_idr, e_cm], chan("s_S"))
        if a == 1 and i == 0:
            Qb.free[qb] = [ev]
            Kb.free[kb] = [ev]
        st = stats[g % 4]
        e1 = put("vector", lambda e: e.tensor_reduce(st[:, i:i + 1], bank[:, 0:n], AX.X, ALU.max, negate=True),
                 [ev] + ([hd[g - 4]["norm"][0]] if g >= 4 else []), chan("s_max"))
        _, Pt, pf = d["P"]

        def rest():
            e2 = put("scalar", lambda e: e.activation(Pt[:, POFF[i]:POFF[i] + n], bank[:, 0:n], ACT.Exp,
                     bias=st[:, i:i + 1], scale=1.0, accum_out=st[:, 4 + i:5 + i]), [e1] + list(pf), chan("s_exp"))
            Sr.free[k] = [e2]
            d["exp"][i] = e2
            if i in (2, 0):
                defer(DN, lambda: normalise(g, i))
        defer(DX, rest)

    def normalise(g, i0):
        d = hd[g]
        st = stats[g % 4]
        er = put("vector", lambda e: e.reciprocal(st[:, 8 + i0:10 + i0], st[:, 4 + i0:6 + i0]), [d["exp"][i0]],
                 chan("s_recip"))
        Pt = d["P"][1]
        for i in (i0 + 1, i0):
            n = 128 * (i + 1)
            ev = put("gpsimd", lambda e, i=i, n=n: e.tensor_scalar(
                Pt[:, POFF[i]:POFF[i] + n], Pt[:, POFF[i]:POFF[i] + n], st[:, 8 + i:9 + i], 1.0,
                ALU.mult, ALU.mult), [er], chan("s_norm"))
            d.setdefault("norm", {})[i] = ev

    GROUPS = [[2], [1, 3], [0]]

    def transposes(g, u):
        d = hd[g]
        pk, Pt, _ = d["P"]
        until(lambda: GROUPS[u][0] in d["norm"] and Tr.ready() and (u > 0 or PTb.ready()))
        if u == 0:
            d["PT"] = PTb.take()
            d["pt_ev"] = {}
        tk, PTt, tf = d["PT"]
        k, bank, bf = Tr.take()
        base = OFF[GROUPS[u][0]]
        at = 0
        for j in GROUPS[u]:
            for i in range(j, 4):
                ev = put("tensor", lambda e, i=i, j=j, at=at: e.transpose(
                    bank[:, at:at + 128], Pt[:, POFF[i] + j * 128:POFF[i] + j * 128 + 128], ident[:, :]),
                    [d["norm"][i], e_id] + list(bf), chan("s_T") if (j == GROUPS[u][-1] and i == 3) else None)
                at += 128
        e1 = copy("scalar", PTt[:, 0, base:base + at], bank[:, 0:at], [ev] + list(tf), chan("s_pthi"))

        def rest():
            e2 = minus("vector", PTt[:, 1, base:base + at], bank[:, 0:at], PTt[:, 0, base:base + at],
                       [e1] + list(tf), chan("s_ptlo"))
            Tr.free[k] = [e2]
            for j in GROUPS[u]:
                d["pt_ev"][j] = e2
        defer(DL, rest)
        if u == 2:
            Pb.free[pk] = [ev]

    def av(g):
        d = hd[g]
        P, a = g // 2, g % 2
        Hf = P // 4
        need(("v", Hf, 3))
        vb, Vt, _, evv = halfV[Hf]
        tk, PTt, _ = d["PT"]
        until(lambda: len(d["pt_ev"]) == 4 and Or.ready() and tmpb.ready() and (a or Yf.ready()))
        k, bank, bf = Or.take()
        n = 0
        for j in range(4):
            w = Vt[:, j, P % 4, a * 128:a * 128 + 128]
            for part in range(2):
                n += 1
                sl = slice(OFF[j], OFF[j] + 512 - 128 * j)
                ev = put("tensor", lambda e, j=j, w=w, part=part, sl=sl, n=n: e.matmul(
                    bank[:, 128 * j:512], w, PTt[:, part, sl], start=n == 1, stop=n == 8),
                    list(bf) + [evv, d["pt_ev"][j]], chan("s_av") if n == 8 else None)
        PTb.free[tk] = [ev]
        if g % 8 == 7:
            Vb.free[vb] = [ev]
        main, other = (slice(0, 64), slice(64, 128)) if a == 0 else (slice(64, 128), slice(0, 64))
        xk, tm, xf = tmpb.take()
        e1 = put("scalar", lambda e: e.activation(tm[main, :], bank[other, :], ACT.Copy), [ev] + list(xf),
                 chan("s_ytmp"))
        if a == 0:
            d["Yf"] = Yf.take()
        else:
            d["Yf"] = hd[g - 1]["Yf"]
        yk, Yt, yfree = d["Yf"]

        def rest():
            e2 = put("vector", lambda e: e.tensor_tensor(Yt[main, :], bank[main, :], tm[main, :], ALU.add),
                     [e1] + list(yfree), chan("s_y"))
            Or.free[k] = [e2]
            tmpb.free[xk] = [e2]
            if a == 1:
                defer(1, lambda: split_y(e2))

        def split_y(e2):
            ok, Yo, of = Yb.take()
            e3 = copy("gpsimd", Yo[:, 0, :], Yt[:, :], [e2] + list(of), chan("s_yhi"))
            e4 = minus("gpsimd", Yo[:, 1, :], Yt[:, :], Yo[:, 0, :], [e3], chan("s_ylo"))
            Yf.free[yk] = [e4]
            Yslot[P] = (ok, Yo, e4)
        defer(1, rest)

    NG = B * H
    bg += ln1(0)
    run_bg(1)
    e_wk = split_weight(stage, flat(Wk, 0), flat(Wk, 1), A["wk"], 2048)
    run_bg(2)
    bg += [proj(0, "k"), proj(0, "q")]
    run_bg(1)
    e_wq = split_weight(stage, flat(Wq, 0), flat(Wq, 1), A["wq"], 2048, scale=0.125)
    run_bg(1)
    bg += [vproj(0, t) for t in range(4)]
    e_wv = split_weight(stage, flat(Wv, 0), flat(Wv, 1), A["wv"], 2048)
    run_bg(1)
    e_wo = split_weight(stage, flat(Wo, 0), flat(Wo, 1), A["wo"], 2048)
    for i in range(2):
        Pb.free[i] = list(stage.free[i])
    e_x1free = list(stage.free[2])
    for g in range(NG + LAG):
        P, a = g // 2, g % 2
        cur, prev = g < NG, 1 <= g <= NG
        if cur and a == 0:
            b = P // 8
            if P + 1 < NG // 2:
                bg[0:0] = [proj(P + 1, "k"), proj(P + 1, "q")]
            if P % 8 == 2 and b + 1 < B:
                ahead = ln1(b + 1)
                bg += ahead[0:1]
            if P % 8 == 3 and b + 1 < B:
                bg += ahead[1:]
            Hf = P // 4 + 1
            if Hf < 2 * B:
                bg.append(vproj(Hf, P % 4))
        for item in ORDER:
            if item == "bg":
                run_bg(1 + (len(bg) > 5))
                continue
            if item[0] == "S" and cur:
                scores(g, int(item[1]))
            elif item[0] == "T" and prev:
                transposes(g - 1, int(item[1]))
            elif item == "AV" and g >= LAG:
                av(g - LAG)
                if (g - LAG) % 4 == 3:
                    bg += [oproj((g - LAG) // 4, 0), oproj((g - LAG) // 4, 1)]
            tick()
    run_bg(len(bg))
    until(lambda: not due)
    cx.close()

    phase = [(chan(n), chan(n).n) for n in sems if sems[n].n]

    w1 = sbf(root, "w1", [128, 2, 2, 1024], f32r)
    w2 = sbf(root, "w2", [128, 2, 2, 1024], f32r)
    s1c = sbf(root, "s1c", [128, 4, 8])
    s3b = sbf(root, "s3b", [128, 256])
    hw = sbf(root, "hw", [128, 2, 8, 1024], f32r)
    rmax = [sbf(root, f"rmax{i}", [128, 16]) for i in range(2)]
    flag = [sbf(root, f"flag{i}", [128, 2]) for i in range(3)]
    XWq = sbf(root, "XWq", [128, 2, 2, 256], f32r)
    kT = sbf(root, "kT", [128, 2, 2, 512], f32r)
    vT = sbf(root, "vT", [128, 4, 2, 256], f32r)
    bqk = sbf(root, "bqk", [128, 2, 2])
    m01 = sbf(root, "m01", [128, 256])
    mneg = sbf(root, "mneg", [128, 256])
    xs = Ring([sbf(root, f"xs{i}", [128, NT, 256]) for i in range(2)])
    xns = Ring([sbf(root, "xns0", [128, NT, 256])])
    XTs = Ring([sbf(root, "XTs0", [128, 2, 2, 512], f32r)])
    qf = Ring([sbf(root, f"qf{i}", [128, 512]) for i in range(2)])
    qT = Ring([sbf(root, "qT0", [128, 2, 2, 512], f32r)])
    sf = Ring([sbf(root, "sf0", [128, 4, 64])])
    pf2 = [sbf(root, f"pf{i}", [128, 4, 128]) for i in range(2)]
    pT = Ring([sbf(root, "pT0", [128, 2, 512], f32r)])
    sm2 = Ring([sbf(root, "sm0", [128, NT, 9])])
    st2 = Ring([sbf(root, "st0", [128, 12])])
    gt = Ring([sbf(root, f"gt{i}", [128, 512]) for i in range(2)])
    go2 = sbf(root, "go", [128, 1024])
    stg = sbf(root, "stg", [128, 1024])
    stage = Ring([t[:, a:a + 512] for t in (stg, go2) for a in (0, 512)] + [t[:, :] for t in qf.tiles])
    cx = ExitStack()
    XWk = sbf(cx, "XWk", [128, 2, 2, 256], f32r)
    XWv = sbf(cx, "XWv", [128, 2, 2, 256], f32r)
    ctr = sbf(cx, "ctr", [128, 2, 2, 512], f32r)
    more = [sbf(cx, f"stage{i}", [128, 1024]) for i in range(4)]
    cx.close()
    Hb = sbf(root, "Hb", [128, 2, 8, 512], f32r)
    fl4 = lambda w, i: w[:, i].rearrange("p k f -> p (k f)")

    for e in Q.q:
        Q.wait(e, phase)
    G8 = Ring(psum)

    X = [{} for _ in range(B)]
    e_x2 = {}

    def xa_load(b):
        d = X[b]
        d["x"] = xs.take()
        d["e_x"] = dma(d["x"][1][:, :, :], x1_v[b], f"s_xs{d['x'][0]}", d["x"][2])

    xa_load(0)
    e_ct = split_weight(stage, fl4(ctr, 0), fl4(ctr, 1), A["ctxT"].rearrange("p k n -> p (k n)"), 1024)
    e_xwk = split_weight(stage, fl4(XWk, 0), fl4(XWk, 1), A["xwk"], 512)
    e_xwq = split_weight(stage, fl4(XWq, 0), fl4(XWq, 1), A["xwq"], 512)
    e_xwv = split_weight(stage, fl4(XWv, 0), fl4(XWv, 1), A["xwv"], 512)
    for i in range(2):
        qf.free[i] = list(stage.free[4 + i])
    stage = Ring([stg[:, :], go2[:, :]] + [t[:, :] for t in more],
                 [stage.free[0] + stage.free[1], stage.free[2] + stage.free[3]] + [list(f) for f in stage.free[2:6]])

    mi = gt.tiles[0][:, 0:256].bitcast(i32)
    bvb = gt.tiles[1][:, 0:256]
    e_mi = dma(mi, A["mask"], "s_mask")
    e_bv = dma(bvb, A["bv"].broadcast_to([128, 256]), "s_bvb")
    e_bqk = dma(bqk[:, :, :], A["bqk"], "s_bqk")
    e_sc = dma(s1c[:, :, :], A["sc"], "s_sc")
    e_s3 = dma(s3b[:, :], A["s3"].broadcast_to([128, 256]), "s_s3")
    def layer2norm(b, key):
        d = X[b]
        d["xn"] = xns.take()
        d["sm"] = sm2.take()
        d["e_xn"] = layernorm(d["x"][1], d["xn"][1], d["sm"][1], [d[key]], d["xn"][2] + d["sm"][2])[0]
        sm2.free[d["sm"][0]] = [d["e_xn"]]

    def xa_ln(b):
        layer2norm(b, "e_x")
        xs.free[X[b]["x"][0]] = [X[b]["e_xn"]]

    def xa_t(b):
        d = X[b]
        d["XT"] = XTs.take()
        d["e_XT"] = [transpose_split(d["xn"][1], d["e_xn"], d["XT"][1], d["XT"][2], G8, j) for j in range(2)]
        xns.free[d["xn"][0]] = d["e_XT"]

    def xa_q(b):
        d = X[b]
        d["qT"] = qT.take()
        Xt = d["XT"][1]
        d["e_q"] = []
        for m in range(2):
            k, bank, bf = G8.take()
            ms = slice(m * 128, m * 128 + 128)
            for c in range(2):
                ev = mm3(bank[:, :], XWq[:, 0, c, ms], XWq[:, 1, c, ms], Xt[:, 0, c, :], Xt[:, 1, c, :],
                         c == 0, c == 1, list(bf) + d["e_XT"] + e_xwq, chan("s_xq") if c else None)
            qk, qt, qfree = qf.take()
            qtt = d["qT"][1]
            e1 = put("vector", lambda e, m=m, bank=bank, qt=qt: e.tensor_scalar(
                qt[:, :], bank[:, :], bqk[:, 0, m:m + 1], None, ALU.add), [ev, e_bqk] + list(qfree), chan("s_xqf"))
            G8.free[k] = [e1]
            e2 = copy("scalar", qtt[:, 0, m, :], qt[:, :], [e1] + d["qT"][2], chan("s_xqhi"))
            e3 = minus("gpsimd", qtt[:, 1, m, :], qt[:, :], qtt[:, 0, m, :], [e2] + d["qT"][2], chan("s_xqlo"))
            qf.free[qk] = [e3]
            d["e_q"].append(e3)
        XTs.free[d["XT"][0]] = [ev]

    def xa_s(b):
        d = X[b]
        k, bank, bf = G8.take()
        qtt = d["qT"][1]
        ks = slice(b * 64, b * 64 + 64)
        for t in range(4):
            ts = slice(t * 128, t * 128 + 128)
            for c in range(2):
                ev = mm3(bank[:, t * 64:t * 64 + 64], qtt[:, 0, c, ts], qtt[:, 1, c, ts], kT[:, 0, c, ks],
                         kT[:, 1, c, ks], c == 0, c == 1, list(bf) + d["e_q"] + ek,
                         chan("s_xS") if (t == 3 and c == 1) else None)
        qT.free[d["qT"][0]] = [ev]
        d["sf"] = sf.take()
        sk, st_, sfree = d["sf"]
        s4 = st_[:, :, :].rearrange("p t k -> p (t k)")
        e1 = put("vector", lambda e: e.tensor_tensor(s4, bank[:, 0:256], m01[:, :], ALU.mult), [ev, e_m] + list(sfree),
                 chan("s_xmask"))
        G8.free[k] = [e1]
        e1 = put("vector", lambda e: e.tensor_tensor(s4, s4, mneg[:, :], ALU.add), [e1], chan("s_xmask"))
        d["st"] = st2.take()
        stt = d["st"][1]
        e1 = put("vector", lambda e: e.tensor_reduce(stt[:, 0:4], st_[:, :, :], AX.X, ALU.max, negate=True),
                 [e1] + list(d["st"][2]), chan("s_xmask"))
        d["e_s"] = e1

    def xa_e(b):
        d = X[b]
        sk, st_, _ = d["sf"]
        tk, stt, _ = d["st"]
        pt = pf2[b % 2]
        o = 64 * (b % 2)
        for t in range(4):
            e2 = put("scalar", lambda e, t=t: e.activation(pt[:, t, o:o + 64], st_[:, t, :], ACT.Exp,
                     bias=stt[:, t:t + 1], scale=1.0, accum_out=stt[:, 4 + t:5 + t]), [d["e_s"]] + pf_free[b % 2],
                     chan("s_xe"))
        sf.free[sk] = [e2]
        e3 = put("vector", lambda e: e.reciprocal(stt[:, 8:12], stt[:, 4:8]), [e2], chan("s_xr"))
        for t in range(4):
            e4 = put("gpsimd", lambda e, t=t: e.tensor_scalar(pt[:, t, o:o + 64], pt[:, t, o:o + 64],
                     stt[:, 8 + t:9 + t], 1.0, ALU.mult, ALU.mult), [e3], chan("s_xn"))
        st2.free[tk] = [e4]
        d["e_p"] = e4

    def xa_pt(b):
        d = X[b]
        d["x"] = xs.take()
        d["e_x"] = dma(d["x"][1][:, :, :], x1_v[b], f"s_xs{d['x'][0]}", d["x"][2])
        pt = pf2[b % 2]
        k, bank, bf = G8.take()
        for t in range(4):
            ev = put("tensor", lambda e, t=t: e.transpose(bank[:, t * 128:t * 128 + 128], pt[:, t, :],
                     ident[:, :]), list(bf) + [d["e_p"]], chan("s_xpT") if t == 3 else None)
        pf_free[b % 2] = [ev]
        d["pT"] = pT.take()
        pk, ptt, pfr = d["pT"]
        e1 = copy("scalar", ptt[:, 0, :], bank[:, :], [ev] + list(pfr), chan("s_xphi"))
        e2 = minus("vector", ptt[:, 1, :], bank[:, :], ptt[:, 0, :], [e1], chan("s_xplo"))
        G8.free[k] = [e2]
        d["e_pT"] = e2

    def xa_o(b):
        d = X[b]
        pk, ptt, _ = d["pT"]
        w = b // 2
        xk, xt, _ = d["x"]
        es = []
        for tt in range(2):
            k, bank, bf = G8.take()
            for t in range(2):
                ts = slice((2 * tt + t) * 128, (2 * tt + t) * 128 + 128)
                ev = mm3(bank[:, t * 256:t * 256 + 256], ptt[:, 0, ts], ptt[:, 1, ts], vT[:, w, 0, :], vT[:, w, 1, :],
                         True, True, list(bf) + [d["e_pT"], ev_[w]], chan("s_xo") if t else None)
            xv = xt[:, 2 * tt:2 * tt + 2, :].rearrange("p t c -> p (t c)")
            e3 = put("vector", lambda e, bank=bank, xv=xv: e.tensor_tensor(xv, xv, bank[:, :], ALU.add),
                     [ev, d["e_x"]], chan("s_xacc2"))
            G8.free[k] = [e3]
            es.append(e3)
        pT.free[pk] = [ev]
        d["e_x2"] = e3
        e_x2[b] = dma(x2_v[b], xt[:, :, :], f"s_x2st{xk}", es)

    def f_ln(b):
        layer2norm(b, "e_x2")
        xs.free[X[b]["x"][0]] = [e_x2[b], X[b]["e_xn"]]


    e1 = put("vector", lambda e: e.tensor_scalar(m01[:, :], mi, 0.0, None, ALU.not_equal), [e_mi], chan("s_m"))
    e_m = put("vector", lambda e: e.tensor_scalar(mneg[:, :], m01[:, :], 1.0, 1e9, ALU.subtract, ALU.mult), [e1],
              chan("s_m"))
    for i in range(2):
        e_pz = put("gpsimd", lambda e, i=i: e.memset(pf2[i][:, :, :], 0.0), (), s_c)
    pf_free = [[e_pz], [e_pz]]
    xa_ln(0)
    xa_load(1)
    ek = []
    for m in range(2):
        k, bank, bf = G8.take()
        ms = slice(m * 128, m * 128 + 128)
        for c in range(2):
            ev = mm3(bank[:, :], XWk[:, 0, c, ms], XWk[:, 1, c, ms], ctr[:, 0, c, :], ctr[:, 1, c, :], c == 0, c == 1,
                     list(bf) + e_xwk + e_ct, chan("s_xk") if c else None)
        qk, qt, qfree = qf.take()
        e1 = put("vector", lambda e, m=m, bank=bank, qt=qt: e.tensor_scalar(qt[:, :], bank[:, :], bqk[:, 1, m:m + 1],
                 None, ALU.add), [ev, e_bqk] + list(qfree), chan("s_xkf"))
        G8.free[k] = [e1]
        e2 = copy("scalar", kT[:, 0, m, :], qt[:, :], [e1], chan("s_xkhi"))
        e3 = minus("vector", kT[:, 1, m, :], qt[:, :], kT[:, 0, m, :], [e2], chan("s_xklo"))
        qf.free[qk] = [e3]
        ek.append(e3)
    xa_t(0)
    xa_q(0)
    ev_ = []
    for w in range(4):
        k, bank, bf = G8.take()
        ws = slice(w * 128, w * 128 + 128)
        for c in range(2):
            ev = mm3(bank[:, 0:256], ctr[:, 0, c, ws], ctr[:, 1, c, ws], XWv[:, 0, c, :], XWv[:, 1, c, :],
                     c == 0, c == 1, list(bf) + e_xwv + e_ct, chan("s_xv") if c else None)
        qk, qt, qfree = qf.take()
        e1 = put("vector", lambda e, bank=bank, qt=qt: e.tensor_tensor(qt[:, 0:256], bank[:, 0:256], bvb, ALU.add),
                 [ev, e_bv] + list(qfree), chan("s_xvf"))
        G8.free[k] = [e1]
        e2 = copy("scalar", vT[:, w, 0, :], qt[:, 0:256], [e1], chan("s_xvhi"))
        e3 = minus("vector", vT[:, w, 1, :], qt[:, 0:256], vT[:, w, 0, :], [e2], chan("s_xvlo"))
        qf.free[qk] = [e3]
        ev_.append(e3)
    e_H = [None] * 8
    H_free = [[ev] for _ in range(8)]
    for i in range(2):
        gt.free[i] = [e_m, e3]

    hwf = lambda i, m: hw[:, i, m, :]
    rm = [rmax[0], 0, None]
    half_w = lambda w, k, n: [w[:, 0, k, :], w[:, 1, k, :], A[n][:, k * 1024:k * 1024 + 1024]]
    e_w1, e_w2, e_h1 = [], [], []
    pieces = [lambda e_w=e_w, w=w, k=k, n=n: e_w.extend(split_weight(stage, *half_w(w, k, n), 1024, rest=rm))
              for e_w, w, n in ((e_w1, w1, "w1"), (e_w2, w2, "w2")) for k in range(2)]
    pieces += [lambda m=m: e_h1.append(split_weight(stage, hwf(0, m), hwf(1, m), A["h1"][m], 1024, rest=rm,
               eng=("scalar", "gpsimd" if m % 2 else "vector")))
               for m in range(8)]
    for n, f in ((0, xa_s), (2, xa_e), (2, xa_pt), (1, xa_o), (0, f_ln), (1, xa_t), (6, None)):
        for _ in range(n):
            pieces.pop(0)()
            if len(pieces) == 8:
                flag_w = rest_flag(rm, flag[2], "s_flag")
        if f:
            f(0)
    for m in range(8):
        H_free[m] = H_free[m] + stage.free[2 + m // 2]
    go_ = Ring([go2[:, 0:512], go2[:, 512:1024]], [list(stage.free[1]), list(stage.free[1])])
    stage = Ring([stg[:, :]], [stage.free[0]])

    regs = [None]

    def load_flag(i, ev):
        def go(e):
            if regs[0] is None:
                regs[0] = e.alloc_register("low_parts")
            e.reg_load(regs[0], flag[i][0:1, 1:2].bitcast(i32))
        put("tensor", go, [ev])

    def product(parts, waits, last_sig, weight_first):
        n = len(parts)

        def mm(e, dst, w, x, start, stop):
            a, b = (w, x) if weight_first else (x, w)
            return e.matmul(dst, a, b, start=start, stop=stop)
        for i, (dst, wh, wl, xh, xl, ws) in enumerate(parts):
            put("tensor", lambda e, dst=dst, wh=wh, xh=xh, i=i: mm(e, dst, wh, xh, i == 0, False),
                list(waits) + list(ws))
            if i < n - 1:
                put("tensor", lambda e, dst=dst, wh=wh, xl=xl: mm(e, dst, wh, xl, False, False))

        def low(e):
            with e.If_ne(regs[0], 0):
                for dst, wh, wl, xh, xl, _ in parts:
                    mm(e, dst, wl, xh, False, False)
        put("tensor", low)
        dst, wh, wl, xh, xl, _ = parts[-1]
        return put("tensor", lambda e: mm(e, dst, wh, xl, False, True), (), last_sig)

    load_flag(2, flag_w)

    def f_w(b, m):
        d = X[b]
        Xt = d["XT"][1]
        ms = slice(m * 128, m * 128 + 128)
        res = []
        for W, ew in ((w1, e_w1), (w2, e_w2)):
            k, bank, bf = G8.take()
            ev = product([(bank[:, :], W[:, 0, c, ms], W[:, 1, c, ms], Xt[:, 0, c, :], Xt[:, 1, c, :], ())
                          for c in range(2)], list(bf) + d["e_XT"] + ew, chan("s_gu"), True)
            res.append((k, bank, ev))
        (k1, bk1, ev1), (k2, bk2, ev2) = res
        if m == 7:
            XTs.free[d["XT"][0]] = [ev2]
        gk, g_, gf = gt.take()
        e1 = put("scalar", lambda e: e.activation(g_[:, :], bk1[:, :], ACT.Silu, scale=s1c[:, 0, m:m + 1]),
                 [ev1, e_sc] + list(gf), chan("s_silu"))
        G8.free[k1] = [e1]
        e2 = put("vector", lambda e: e.scalar_tensor_tensor(g_[:, :], bk2[:, :], s1c[:, 1, m:m + 1], g_[:, :],
                 ALU.mult, ALU.mult), [ev2, e1, e_sc], chan("s_h"))
        G8.free[k2] = [e2]
        e3 = copy("gpsimd" if m in (0, 2, 4) else "scalar", Hb[:, 0, m, :], g_[:, :], [e2] + H_free[m],
                  chan("s_hhi0" if m in (0, 2, 4) else "s_hhi1"))
        e4 = minus("vector", Hb[:, 1, m, :], g_[:, :], Hb[:, 0, m, :], [e3] + H_free[m], chan("s_hlo"))
        gt.free[gk] = [e4]
        e_H[m] = e4

    def hidden(m, e_h, src, e_in):
        k, bank, bf = G8.take()
        sl = [slice(c * 128, c * 128 + 128) for c in range(8)]
        ev = product([(bank[:, :], hw[:, 0, m, sl[c]], hw[:, 1, m, sl[c]], src[0][:, c, :], src[1][:, c, :],
                       [e_in[c]]) for c in range(8)], list(bf) + e_h[m], chan("s_hid"), True)
        return k, bank, ev

    e_hst = {}

    def f_h(b, m):
        k, bank, ev = hidden(m, e_h1, (Hb[:, 0], Hb[:, 1]), e_H)
        if m == 7:
            for c in range(8):
                H_free[c] = [ev]
        ok, o_, of = go_.take()
        e1 = put("scalar", lambda e: e.activation(o_, bank[:, :], ACT.Gelu, scale=s1c[:, 2, m:m + 1]),
                 [ev] + list(of), chan("s_gelu"))
        G8.free[k] = [e1]
        e_hst[b, m] = dma(h_d[b, m], o_, f"s_hst{ok}", [e1])
        go_.free[ok] = [e_hst[b, m]]
        return ev

    rm2 = [rmax[1], 0, None]

    seen = {}

    def look_load(src):
        k, st, free = stage.take()
        seen["now"] = (k, st, dma(st, src, "s_look", list(free)))

    def look(k, st, e_ld):
        bits = st.bitcast(i32)
        e_and = put("vector", lambda e: e.tensor_scalar(bits, bits, 0xFFF, None, ALU.bitwise_and), [e_ld],
                    chan("s_rest"))
        stage.free[k] = [largest(rm2, bits, [e_and])]

    looks = [A["h2"][m] for m in range(8)] + [A["w3"][:, 0:1024], A["w3"][:, 1024:2048]]

    AT = {("w", 7): [xa_t], ("h", 0): [xa_q], ("h", 1): [xa_s, xa_e], ("h", 3): [xa_pt],
          ("h", 4): [xa_o, f_ln], ("h", 6): [xa_t]}

    def xa_first(b):
        xa_ln(b)
        if b + 1 < B:
            xa_load(b + 1)

    def f_batch(b):
        def stages(*at):
            for f in AT.get(at, ()) if b + 1 < B else ():
                f(b + 1)
            if at == ("h", 7) and b + 2 < B:
                xa_first(b + 2)
        for m in range(8):
            f_w(b, m)
            stages("w", m)
        if b == 0:
            load_flag(0, rest_flag(rm, flag[0], "s_flag"))
        for m in range(8):
            e_hw_last[m] = f_h(b, m)
            stages("h", m)
            if b in (1, 2, 3) and m % 2 == 0 and looks:
                look_load(looks.pop(0))
            if m % 2 == 1 and "now" in seen:
                look(*seen.pop("now"))
            yield m

    e_hw_last = [None] * 8
    xa_first(1)
    for b in range(B - 1):
        for _ in f_batch(b):
            pass
    load2 = rest_flag(rm2, flag[1], "s_flag")

    Gb = [w[:, :, :, :].rearrange("p a k f -> p (a k f)").rearrange("p (c n) -> p c n", c=8) for w in (w1, w2)]
    hl = Ring([t[:, :] for t in qf.tiles] + [t[:, :, :].rearrange("p t k -> p (t k)") for t in pf2],
              qf.free + pf_free)
    w3 = [t[:, :, :, :].rearrange("p a b n -> p (a b n)").rearrange("p (c n) -> p c n", c=8) for t in (kT, vT)]
    xnf = xns.tiles[0][:, :, :].rearrange("p t c -> p (t c)")
    xsf = xs.tiles[0][:, :, :].rearrange("p t c -> p (t c)")
    e_G = [None] * 8

    def g_fetch(b, m):
        k, t, f = hl.take()
        fetched[m] = (k, t, dma(t, h_d[b, m], f"s_hl{k}", list(f) + [e_hst[b, m]]))

    def g_split(m):
        k, t, e0 = fetched.pop(m)
        e1 = copy("gpsimd", Gb[0][:, m, :], t, [e0] + G_free[m], chan("s_h2hi"))
        e2 = minus("vector", Gb[1][:, m, :], t, Gb[0][:, m, :], [e1] + G_free[m], chan("s_h2lo"))
        hl.free[k] = [e2]
        e_G[m] = e2
    fetched = {}

    kv_free = [(chan(n), chan(n).n) for n in ("s_xS", "s_xo")]
    ot = Ring([xnf[:, 0:512], xnf[:, 512:1024]], [list(xns.free[0]), list(xns.free[0])])
    stage2 = Ring([stg[:, :], xsf], [list(stage.free[0]), list(xs.free[0])])
    e_w3 = split_weight(stage2, w3[0].rearrange("p c n -> p (c n)"), w3[1].rearrange("p c n -> p (c n)"),
                        A["w3"], 2048, after=kv_free)
    e_h2, w_at = [], {}

    def w_fetch(m):
        k, st, free = stage2.take()
        w_at[m] = (k, st, dma(st, A["h2"][m], f"s_wld{k}", list(free)))

    def w_split(m):
        k, st, e_ld = w_at.pop(m)
        e_hi = copy("scalar", hwf(0, m), st, [e_ld, e_hw_last[m]], chan("s_whi_scalar"))
        e_lo = minus("vector", hwf(1, m), st, hwf(0, m), [e_hi, e_hw_last[m]], chan("s_wlo_vector"))
        stage2.free[k] = [e_lo]
        e_h2.append([e_lo])

    for m in range(4):
        g_fetch(0, m)
    w_fetch(0)
    w_fetch(1)
    for m in f_batch(B - 1):
        if m == 0:
            G_free = [[(chan("s_gu"), chan("s_gu").n)] for _ in range(8)]
        else:
            w_split(m - 1)
            if m < 7:
                w_fetch(m + 1)
        g_split(m)
        if m < 4:
            g_fetch(0, m + 4)
    w_split(7)
    load_flag(1, load2)
    xs = Ring([xs.tiles[1]], [list(xs.free[1])])

    def g_h(m):
        k, bank, ev = hidden(m, e_h2, Gb, e_G)
        if m == 7:
            for c in range(8):
                G_free[c] = [ev]
        gk, g_, gf = gt.take()
        e1 = put("scalar", lambda e: e.activation(g_[:, :], bank[:, :], ACT.Gelu, scale=s1c[:, 3, m:m + 1]),
                 [ev] + list(gf), chan("s_gelu2"))
        G8.free[k] = [e1]
        e2 = copy("scalar", Hb[:, 0, m, :], g_[:, :], [e1] + H_free[m], chan("s_ghi"))
        e3 = minus("vector", Hb[:, 1, m, :], g_[:, :], Hb[:, 0, m, :], [e2] + H_free[m], chan("s_glo"))
        gt.free[gk] = [e3]
        e_H[m] = e3

    xg = {}

    def g_out(b, tt):
        k, bank, bf = G8.take()
        for t in range(2):
            ts = slice((2 * tt + t) * 128, (2 * tt + t) * 128 + 128)
            ev = product([(bank[:, t * 256:t * 256 + 256], w3[0][:, c, :], w3[1][:, c, :], Hb[:, 0, c, ts],
                           Hb[:, 1, c, ts], [e_H[c]]) for c in range(8)], list(bf) + e_w3, chan("s_out"), False)
        if tt == 1:
            for c in range(8):
                H_free[c] = [ev]
        ok, o_, of = ot.take()
        for t in range(2):
            e1 = put("vector", lambda e, t=t: e.tensor_tensor(o_[:, t * 256:t * 256 + 256],
                     bank[:, t * 256:t * 256 + 256], s3b[:, :], ALU.mult), [ev, e_s3] + list(of), chan("s_fs"))
        G8.free[k] = [e1]
        xk, xt, _, ex = xg[b]
        xv = xt[:, 2 * tt:2 * tt + 2, :].rearrange("p t c -> p (t c)")
        e2 = put("vector", lambda e: e.tensor_tensor(o_, o_, xv, ALU.add), [e1, ex], chan("s_fs"))
        e3 = dma(out_v[b][:, 2 * tt:2 * tt + 2, :], o_.rearrange("p (t c) -> p t c", t=2), f"s_final{ok}", [e2])
        ot.free[ok] = [e3]
        if tt == 1:
            xs.free[xk] = [e2]

    for b in range(B):
        k, t, f = xs.take()
        xg[b] = (k, t, f, dma(t[:, :, :], x2_v[b], "s_xg", list(f) + [e_x2[b]]))
        for m in range(8):
            g_h(m)
        if b + 1 < B:
            for m in range(8):
                g_fetch(b + 1, m)
                g_split(m)
        g_out(b, 0)
        g_out(b, 1)
    Q.wait("sync", [(c, c.n) for n, c in sems.items() if n[:-1] in ("s_final", "s_x1st", "s_x2st", "s_hst")])

    with nc.Block() as block:
        @block.sync
        def _(e):
            for f in Q.q["sync"]:
                f(e)

        @block.gpsimd
        def _(e):
            for f in Q.q["gpsimd"]:
                f(e)

        @block.scalar
        def _(e):
            for f in Q.q["scalar"]:
                f(e)

        @block.vector
        def _(e):
            for f in Q.q["vector"]:
                f(e)

        @block.tensor
        def _(e):
            for f in Q.q["tensor"]:
                f(e)
    root.close()


def kernel(**inputs):
    import numpy as np
    import concourse.bacc as _bacc
    from concourse import mybir as _mybir
    from concourse.bass_utils import run_bass_kernel_spmd as _run

    I = {k: np.asarray(v) for k, v in inputs.items()}

    def kt(w):
        o, i = w.shape
        return w.T.reshape(i // 128, 128, o).transpose(1, 0, 2).reshape(128, -1)

    def mkt(w):
        o, i = w.shape
        return w.T.reshape(i // 128, 128, o // 128, 128).transpose(2, 1, 0, 3).reshape(o // 128, 128, i)

    col = lambda v: v.reshape(-1, 128).T
    a = {
        "x": I["x"],
        "wq": kt(I["L0_attn_w_q"].reshape(1024, 256)),
        "wk": kt(I["L0_attn_w_k"].reshape(1024, 256)),
        "wv": kt(I["L0_attn_w_v"].reshape(1024, 256)),
        "wo": kt(I["L0_attn_w_o"].T),
        "xwq": kt(I["L0_xattn_Wq"]),
        "xwk": kt(I["L0_xattn_Wk"]),
        "xwv": kt(I["L0_xattn_Wv"]),
        "bqk": np.stack([col(I["L0_xattn_bq"]), col(I["L0_xattn_bk"])], 1),
        "bv": I["L0_xattn_bv"].reshape(1, 256),
        "ctxT": I["ctx_1024"].reshape(512, 256).T.reshape(2, 128, 512).transpose(1, 0, 2),
        "mask": I["mask_SxS2_ik1"].reshape(4, 128, 64).transpose(1, 0, 2).reshape(128, 256),
        "w1": kt(I["L0_ffn_w1_w"]),
        "w2": kt(I["L0_ffn_w2_w"]),
        "h1": mkt(I["L0_ffn_h1_w"]),
        "h2": mkt(I["L0_ffn_h2_w"]),
        "w3": kt(I["L0_ffn_w3_w"]),
        "sc": np.stack([col(I[f"L0_ffn_{n}_s"]) for n in ("w1", "w2", "h1", "h2")], 1),
        "s3": I["L0_ffn_w3_s"].reshape(1, 256),
    }
    a = {k: np.ascontiguousarray(v) for k, v in a.items()}
    nc = _bacc.Bacc("TRN2", target_bir_lowering=False, num_devices=1)
    aps = {k: nc.dram_tensor(f"in_{k}", v.shape, _mybir.dt.from_np(v.dtype), kind="ExternalInput").ap()
           for k, v in a.items()}
    out = nc.dram_tensor("out_0", (B, T, C), _mybir.dt.float32, kind="ExternalOutput").ap()
    program(nc, aps, out)
    r = _run(nc, [{f"in_{k}": v for k, v in a.items()}], core_ids=[0])
    return r.results[0]["out_0"]
```
